# Optimizing a Trainium2 kernel written in Bass

```python
import numpy as np
import jax
import jax.numpy as jnp

def _softmax(x, axis=-1):
    return jax.nn.softmax(x, axis=axis)

def _gelu(x):
    return jax.nn.gelu(x, approximate=True)

def _silu(x):
    return jax.nn.silu(x)

def _sigmoid(x):
    return jax.nn.sigmoid(x)

def _layernorm(x, axis=-1, eps=1e-05):
    m = jnp.mean(x, axis=axis, keepdims=True)
    v = jnp.var(x, axis=axis, keepdims=True)
    return (x - m) / jnp.sqrt(v + eps)

def _scatter_add(tgt, idx, src, axis=0):
    return tgt.at[idx].add(src)

def _segment_sum(src, seg, n):
    return jax.ops.segment_sum(src, seg, n)
kernel_name = 'mk_dlrm_tower_d1_rec_r8_a4c6dd'

def setup_inputs(seed: int=0):
    np.random.seed(seed)
    _w = jnp.asarray

    def _rec_inputs():
        import jax
        import jax.numpy as jnp
        _tk = jax.random.key(seed)
        dense_ctx = jax.random.normal(jax.random.fold_in(_tk, 190), (2048, 16), jnp.float32)
        ids = jnp.stack([jax.random.randint(jax.random.fold_in(_tk, 200 + f), (2048,), 0, v, jnp.int32) for f, v in enumerate([1000, 1250, 125000, 12500, 1250, 1250, 12500, 125000, 12500, 1000, 125000, 12500, 12500, 125000, 125000, 1000])], axis=1)
        tbl_0 = 0.05 * jax.random.normal(jax.random.fold_in(_tk, 500 + 0), (1000, 16), jnp.float32)
        tbl_1 = 0.05 * jax.random.normal(jax.random.fold_in(_tk, 500 + 1), (1250, 16), jnp.float32)
        tbl_2 = 0.05 * jax.random.normal(jax.random.fold_in(_tk, 500 + 2), (125000, 16), jnp.float32)
        tbl_3 = 0.05 * jax.random.normal(jax.random.fold_in(_tk, 500 + 3), (12500, 16), jnp.float32)
        tbl_4 = 0.05 * jax.random.normal(jax.random.fold_in(_tk, 500 + 4), (1250, 16), jnp.float32)
        tbl_5 = 0.05 * jax.random.normal(jax.random.fold_in(_tk, 500 + 5), (1250, 16), jnp.float32)
        tbl_6 = 0.05 * jax.random.normal(jax.random.fold_in(_tk, 500 + 6), (12500, 16), jnp.float32)
        tbl_7 = 0.05 * jax.random.normal(jax.random.fold_in(_tk, 500 + 7), (125000, 16), jnp.float32)
        tbl_8 = 0.05 * jax.random.normal(jax.random.fold_in(_tk, 500 + 8), (12500, 16), jnp.float32)
        tbl_9 = 0.05 * jax.random.normal(jax.random.fold_in(_tk, 500 + 9), (1000, 16), jnp.float32)
        tbl_10 = 0.05 * jax.random.normal(jax.random.fold_in(_tk, 500 + 10), (125000, 16), jnp.float32)
        tbl_11 = 0.05 * jax.random.normal(jax.random.fold_in(_tk, 500 + 11), (12500, 16), jnp.float32)
        tbl_12 = 0.05 * jax.random.normal(jax.random.fold_in(_tk, 500 + 12), (12500, 16), jnp.float32)
        tbl_13 = 0.05 * jax.random.normal(jax.random.fold_in(_tk, 500 + 13), (125000, 16), jnp.float32)
        tbl_14 = 0.05 * jax.random.normal(jax.random.fold_in(_tk, 500 + 14), (125000, 16), jnp.float32)
        tbl_15 = 0.05 * jax.random.normal(jax.random.fold_in(_tk, 500 + 15), (1000, 16), jnp.float32)
        _rk = jax.random.fold_in(_tk, 7)
        r_x0 = -0.000233584 + 0.999828 * jax.random.normal(jax.random.fold_in(_rk, 101), (2048, 39, 16), jnp.float32)
        W_top1 = 0.0606339 * jax.random.normal(jax.random.fold_in(_tk, 801), (272, 512), jnp.float32)
        W_top2 = 0.0441942 * jax.random.normal(jax.random.fold_in(_tk, 802), (512, 256), jnp.float32)
        W_top3 = 0.0625 * jax.random.normal(jax.random.fold_in(_tk, 803), (256, 1), jnp.float32)
        b_top1 = jnp.zeros((512,), jnp.float32)
        b_top2 = jnp.zeros((256,), jnp.float32)
        return (dense_ctx, ids, tbl_0, tbl_1, tbl_2, tbl_3, tbl_4, tbl_5, tbl_6, tbl_7, tbl_8, tbl_9, tbl_10, tbl_11, tbl_12, tbl_13, tbl_14, tbl_15, r_x0, W_top1, b_top1, W_top2, b_top2, W_top3)
    dense_ctx, ids, tbl_0, tbl_1, tbl_2, tbl_3, tbl_4, tbl_5, tbl_6, tbl_7, tbl_8, tbl_9, tbl_10, tbl_11, tbl_12, tbl_13, tbl_14, tbl_15, r_x0, W_top1, b_top1, W_top2, b_top2, W_top3 = _rec_inputs()

    def _L0_rec_setup():
        import jax, jax.numpy as jnp
        import numpy as np
        B, S, F, D, K = (1024, 16, 39, 16, 16)
        key = jax.random.key(seed)
        k1, k2, k3, k4, k5 = jax.random.split(key, 5)
        xl = jax.random.normal(k1, (B, S, D), dtype=jnp.float32)
        x0 = jax.random.normal(k2, (B, F, D), dtype=jnp.float32)
        w = jnp.broadcast_to(jnp.eye(D, dtype=jnp.float32), (K, D, D)) + 0.02 * jax.random.normal(k3, (K, D, D), dtype=jnp.float32)
        alpha = jnp.ones((S * F, K), dtype=jnp.float32) + 0.02 * jax.random.normal(k4, (S * F, K), dtype=jnp.float32)
        hv = jnp.ones((K, D, 1), dtype=jnp.float32) + 0.02 * jax.random.normal(k5, (K, D, 1), dtype=jnp.float32)
        return {'xl': xl, 'x0': x0, 'w': w, 'alpha': alpha, 'hv': hv}
    _L0_rec_all = _L0_rec_setup()
    _L0_rec_in = {k: v for k, v in _L0_rec_all.items() if k in ('w', 'alpha', 'hv')}
    del _L0_rec_all
    return {'dense_ctx': dense_ctx, 'ids': ids, 'tbl_0': tbl_0, 'tbl_1': tbl_1, 'tbl_2': tbl_2, 'tbl_3': tbl_3, 'tbl_4': tbl_4, 'tbl_5': tbl_5, 'tbl_6': tbl_6, 'tbl_7': tbl_7, 'tbl_8': tbl_8, 'tbl_9': tbl_9, 'tbl_10': tbl_10, 'tbl_11': tbl_11, 'tbl_12': tbl_12, 'tbl_13': tbl_13, 'tbl_14': tbl_14, 'tbl_15': tbl_15, 'r_x0': r_x0, 'W_top1': W_top1, 'b_top1': b_top1, 'W_top2': W_top2, 'b_top2': b_top2, 'W_top3': W_top3, 'L0_rec_w': _L0_rec_in['w'], 'L0_rec_alpha': _L0_rec_in['alpha'], 'L0_rec_hv': _L0_rec_in['hv']}

def reference(dense_ctx, ids, tbl_0, tbl_1, tbl_2, tbl_3, tbl_4, tbl_5, tbl_6, tbl_7, tbl_8, tbl_9, tbl_10, tbl_11, tbl_12, tbl_13, tbl_14, tbl_15, r_x0, W_top1, b_top1, W_top2, b_top2, W_top3, L0_rec_w, L0_rec_alpha, L0_rec_hv):
    import jax
    import jax.numpy as jnp

    def _L0_rec_ref(xl, x0, w, alpha, hv):
        import jax, jax.numpy as jnp
        import numpy as np
        B, S, F, D, K = (1024, 16, 39, 16, 16)
        b, s, d = xl.shape
        f = x0.shape[1]
        A = jnp.repeat(x0, s, axis=1)
        Bm = jnp.repeat(xl, f, axis=2).reshape(b, s * f, d)
        out = jnp.einsum('bnh,bnd,nk,khd,kd->bkh', A, Bm, alpha, w, hv[..., 0])
        return out
    e = jnp.stack([tbl_0[ids[:, 0]], tbl_1[ids[:, 1]], tbl_2[ids[:, 2]], tbl_3[ids[:, 3]], tbl_4[ids[:, 4]], tbl_5[ids[:, 5]], tbl_6[ids[:, 6]], tbl_7[ids[:, 7]], tbl_8[ids[:, 8]], tbl_9[ids[:, 9]], tbl_10[ids[:, 10]], tbl_11[ids[:, 11]], tbl_12[ids[:, 12]], tbl_13[ids[:, 13]], tbl_14[ids[:, 14]], tbl_15[ids[:, 15]]], axis=1)
    z = _L0_rec_ref(e, r_x0, L0_rec_w, L0_rec_alpha, L0_rec_hv)
    z = z.reshape(z.shape[0], -1)
    h = jnp.concatenate([z, dense_ctx], axis=1)
    h = jnp.maximum(h @ W_top1 + b_top1, 0.0)
    h = jnp.maximum(h @ W_top2 + b_top2, 0.0)
    y = h @ W_top3
    return y

_drawn_inputs = setup_inputs


def setup_inputs(seed=0):
    import zlib

    import numpy as np

    out = dict(_drawn_inputs(seed))
    spreads = {'b_top1': (0.0, 0.1), 'b_top2': (0.0, 0.1)}
    factors = {}
    for name, (base, spread) in spreads.items():
        noise = np.random.default_rng([zlib.crc32(name.encode()), seed]).standard_normal(out[name].shape)
        drawn = base * np.exp(spread * noise) if base else spread * noise
        out[name] = jnp.asarray(drawn.astype(out[name].dtype))
    for name, factor in factors.items():
        out[name] = (out[name] * factor).astype(out[name].dtype)
    return out
```

```python
import concourse.bass as bass
from concourse import mybir
from contextlib import ExitStack

F32 = mybir.dt.float32
BF16 = mybir.dt.bfloat16
I32 = mybir.dt.int32
ALU = mybir.AluOpType
ACT = mybir.ActivationFunctionType
AX = mybir.AxisListType

P = 128
B = 2048
NT, D = 16, 16
NE = NT * D
F, H, K = 39, 16, 16
NW = 8
N1, N2 = 512, 256
SUB = 2
W = SUB * P
STEPS = B // W
PAIRS = STEPS // 2
NXR, NSC = 4, 3
QUADS = H // 4
PB = 5 * QUADS
HALF = PB // 2
X3 = 3 * F

C_ID, C_SE, C_SX, C_MK, C_BD = 0, 128, 128 + 4 * 128, 128 + 7 * 128, 128 + 7 * 128 + 3 * 256
C_END = C_BD + 2 * 16
SE_TERMS = [(0, 0), (1, 0), (1, 1), (2, 1)]


def interaction_tower(nc, T, out):
    with ExitStack() as ctx:
        def sb(name, shape, dt=F32):
            return ctx.enter_context(nc.sbuf_tensor(name, shape, dt))

        def sem(name):
            return ctx.enter_context(nc.semaphore(name))

        const = sb("const", [P, C_END])
        ident = const[:, C_ID:C_ID + P]
        sel_e = const[:, C_SE:C_SE + 4 * P].rearrange("p (t r) -> p t r", t=4)
        sel_x32 = const[:, C_SX:C_SX + 3 * P].rearrange("p (c r) -> p c r", c=3)
        mask = const[:, C_MK:C_MK + 3 * 256].rearrange("p (c q) -> p c q", c=3)
        bd_mask = const[:, C_BD:C_BD + 32].rearrange("p (a k) -> p a k", a=2)
        ident_b = sb("ident_b", [P, P], BF16)
        sel_x = sb("sel_x", [P, 3, P], BF16)
        alpha_f = sb("alpha_f", [F, 256])
        alpha_rows = sb("alpha_rows", [P, 3, 256])
        al_terms = sb("al_terms", [P, 256, 16])
        al = sb("al", [P, 3, 256])
        al_t = sb("al_t", [P, 6, P])
        w_t = sb("w_t", [P, 2, H])
        hv_t = sb("hv_t", [P, 2])
        w_diag = sb("w_diag", [P, 2, H * K])
        c01 = sb("c01", [P, 2, H, 32])
        c2 = sb("c2", [P, H // 2, 32])
        w1 = sb("w1", [P, 2, N1])
        w1d = sb("w1d", [D, N1])
        w2 = sb("w2", [P, N1 // P, N2])
        w3 = sb("w3", [P, N2 // P])
        b1 = sb("b1", [P, N1 // P])
        b2 = sb("b2", [P, N2 // P])
        ids = [sb(f"ids{u}", [P, SUB, NT], I32) for u in range(2)]
        x_in = [sb(f"x_in{u}", [P, SUB, F * H]) for u in range(2)]
        e_nat = [sb(f"e_nat{u}", [P, SUB, NE + D]) for u in range(2)]
        x_parts = sb("x_parts", [P, SUB, H, 3, F], BF16)
        x_rest = sb("x_rest", [P, SUB, H, F])
        x_t = sb("x_t", [X3, H, W], BF16)
        e_t = sb("e_t", [P, 2, W])
        dense_t = sb("dense_t", [D, W])
        e_rep = sb("e_rep", [P, 3, W])
        prod = sb("prod", [P, PB, 2 * W])
        z = sb("z", [P, 2, W])
        h1 = sb("h1", [P, N1 // P, W])
        h2 = sb("h2", [P, N2 // P, W])
        y = sb("y", [1, B])

        xr = [ctx.enter_context(nc.psum_tensor(f"xr{k}", [P, 512], F32)) for k in range(NXR)]
        sc = [ctx.enter_context(nc.psum_tensor(f"sc{k}", [P, 512], F32)) for k in range(NSC)]
        zp = ctx.enter_context(nc.psum_tensor("zp", [P, 512], F32))

        const_in, wts_in, mlp_in = sem("const_in"), sem("wts_in"), sem("mlp_in")
        ids_in = [sem(f"ids_in{u}") for u in range(2)]
        x_loaded = [sem(f"x_loaded{u}") for u in range(2)]
        dense_in = [sem(f"dense_in{u}") for u in range(2)]
        gathered = [sem(f"gathered{u}") for u in range(2)]
        e_read = [sem(f"e_read{u}") for u in range(2)]
        y_out = sem("y_out")
        y_turn = sem("y_turn")
        turn = sem("turn")
        casts = sem("casts")
        zeroed = sem("zeroed")
        diag_ready = sem("diag_ready")
        arow_mm, arow_ready = sem("arow_mm"), sem("arow_ready")
        al_step, al_ready = sem("al_step"), sem("al_ready")
        alt_mm, alt_ready = sem("alt_mm"), sem("alt_ready")
        c_mm, c_ready = sem("c_mm"), sem("c_ready")
        hi_done, rest_done, mid_done, lo_done = sem("hi_done"), sem("rest_done"), sem("mid_done"), sem("lo_done")
        sc_full = [sem(f"sc_full{k}") for k in range(NSC)]
        sc_free = [sem(f"sc_free{k}") for k in range(NSC)]
        xr_full = [sem(f"xr_full{k}") for k in range(NXR)]
        mult = [sem(f"mult{k}") for k in range(NXR)]
        contracted = [sem(f"contracted{a}") for a in range(2)]
        z_ready = sem("z_ready")

        ONE = 1

        USES = ["dense", "eT", "e01", "e2", "x0", "a0", "a1", "x1", "a2", "a3", "x2", "b0", "b1", "x3", "y"]
        USES_LAST = [n for n in USES if n[0] != "x"]
        assert len(USES) % NSC == 0
        PER_SC = len(USES) // NSC
        PER_XR = PB // NXR

        PRO = [sum(1 for g in range(QUADS) if g % NSC == k) for k in range(NSC)]
        BANK_ET = USES.index("eT") % NSC

        def scratch(name, last):
            n = (USES_LAST if last else USES).index(name)
            return n % NSC, n // NSC

        def free_before(name, s, last):
            k, q = scratch(name, last)
            return PER_SC * s + q + PRO[k]

        def free_after(name, s, last):
            return free_before(name, s, last) + 1

        def full_after(name, s, last):
            k, q = scratch(name, last)
            mine = int(k == BANK_ET)
            return (PER_SC - mine) * s + q + 1 - mine + PRO[k]

        x_dram = T["r_x0"].rearrange("(s j p) f h -> p s j (f h)", p=P, j=SUB)
        ids_dram = T["ids"].rearrange("(s j p) t -> p s j t", p=P, j=SUB)
        dense_dram = T["dense_ctx"].rearrange("(s j p) c -> p s j c", p=P, j=SUB)

        block = ctx.enter_context(nc.Block())

        @block.sync
        def _(sp):
            def load_ids(s, u):
                sp.dma_start(ids[u][:], ids_dram[:, bass.ds(s, 1)].rearrange("p o j t -> p (o j) t")).then_inc(ids_in[u], 16)

            def load_x(s, u):
                sp.dma_start(x_in[u][:], x_dram[:, bass.ds(s, 1)].rearrange("p o j c -> p (o j) c")).then_inc(x_loaded[u], 16)

            def load_dense(s, u):
                sp.dma_start(e_nat[u][:, :, NE:], dense_dram[:, bass.ds(s, 1)].rearrange("p o j c -> p (o j) c")).then_inc(dense_in[u], 16)

            load_ids(0, 0)
            sp.dma_start(const[:], T["const"]).then_inc(const_in, 16)
            load_x(0, 0)
            load_ids(1, 1)
            sp.dma_start(alpha_f[:], T["L0_rec_alpha"].rearrange("(f j) k -> f (j k)", f=F)).then_inc(wts_in, 16)
            with nc.allow_non_contiguous_dma(reason="w, hv and biases go to partitions element by element, once"):
                for a in range(2):
                    for kk in range(8):
                        sp.dma_start(w_t[16 * kk:16 * kk + 16, a, :],
                                     T["L0_rec_w"][8 * a + kk].rearrange("h d -> d h")).then_inc(wts_in, 16)
                sp.dma_start(hv_t[:], T["L0_rec_hv"].rearrange("(a k) d o -> (k d) (a o)", a=2)).then_inc(wts_in, 16)
                sp.dma_start(b1[:], T["b_top1"].rearrange("(m p) -> p m", p=P)).then_inc(mlp_in, 16)
                sp.dma_start(b2[:], T["b_top2"].rearrange("(m p) -> p m", p=P)).then_inc(mlp_in, 16)
                sp.dma_start(w3[:], T["W_top3"].rearrange("(m p) o -> p (m o)", p=P)).then_inc(mlp_in, 16)
            load_dense(0, 0)
            load_x(1, 1)
            load_dense(1, 1)
            w1_dram = T["W_top1"][0:NE].rearrange("(k a h) n -> h k a n", a=2, h=8)
            for hh in range(8):
                sp.dma_start(w1[16 * hh:16 * hh + 16], w1_dram[hh]).then_inc(mlp_in, 16)
            sp.dma_start(w1d[:], T["W_top1"][NE:NE + D]).then_inc(mlp_in, 16)
            sp.dma_start(w2[:], T["W_top2"].rearrange("(c p) n -> p c n", p=P)).then_inc(mlp_in, 16)
            with sp.Fori(1, PAIRS) as i:
                for u in range(2):
                    sp.wait_ge(gathered[u], 16 * SUB * NT * i)
                    load_ids(2 * i + u, u)
                    sp.wait_ge(rest_done, 2 * i + u - 1)
                    load_x(2 * i + u, u)
                    sp.wait_ge(e_read[u], i + ONE)
                    load_dense(2 * i + u, u)
        WTS, MLP = 16 * 18, 16 * 13

        @block.gpsimd
        def _(pool):
            with pool.Fori(0, PAIRS) as i:
                for u in range(2):
                    pool.wait_ge(ids_in[u], 16 * i + 16)
                    pool.wait_ge(e_read[u], i + ONE)
                    pool.sem_inc(turn, 1)
                    for j in range(SUB):
                        for f in range(NT):
                            nc.gpsimd.indirect_dma_start(
                                e_nat[u][:, j, f * D:(f + 1) * D], None, T[f"tbl_{f}"],
                                bass.IndirectOffsetOnAxis(ap=ids[u][:, j, f:f + 1], axis=0)).then_inc(gathered[u], 16)

        @block.scalar
        def _(act):
            def hi(i, u):
                act.wait_ge(x_loaded[u], 16 * i + 16)
                nc.scalar.activation(x_parts[:, :, :, 0, :], x_in[u][:].rearrange("p j (f h) -> p j h f", h=H),
                                     ACT.Copy).then_inc(hi_done, 1)

            def mid(s):
                act.wait_ge(rest_done, s + 1)
                nc.scalar.activation(x_parts[:, :, :, 1, :], x_rest[:], ACT.Copy).then_inc(mid_done, 1)

            def xt_evac(s, g, k, n):
                act.wait_ge(sc_full[k], n)
                nc.scalar.activation(x_t[:, 4 * g:4 * g + 4, :], sc[k][0:X3, :].bitcast(BF16).rearrange("p (h n) -> p h n", h=4),
                                     ACT.Copy).then_inc(sc_free[k], 1)

            act.sem_inc(z_ready, ONE)
            act.wait_ge(const_in, 16)
            nc.scalar.activation(ident_b[:], ident, ACT.Copy).then_inc(casts, 1)
            nc.scalar.activation(sel_x[:], sel_x32, ACT.Copy).then_inc(casts, 1)
            hi(0, 0)
            for c in range(3):
                act.wait_ge(arow_mm, c + 1)
                nc.scalar.activation(alpha_rows[:, c, :], xr[c][:, 0:256], ACT.Copy).then_inc(arow_ready, 1)
            mid(0)
            for g in range(QUADS):
                act.wait_ge(sc_full[g % NSC], g // NSC + 1)
                nc.scalar.activation(x_t[:, 4 * g:4 * g + 4, :], sc[g % NSC][0:X3, :].bitcast(BF16).rearrange("p (h n) -> p h n", h=4),
                                     ACT.Copy).then_inc(sc_free[g % NSC], 1)
            act.wait_ge(alt_mm, 1)
            nc.scalar.activation(al_t[:, 0:4, :], xr[0][:].rearrange("p (t r) -> p t r", t=4), ACT.Copy).then_inc(alt_ready, 1)
            act.wait_ge(alt_mm, 2)
            nc.scalar.activation(al_t[:, 4:6, :], xr[1][:, 0:256].rearrange("p (t r) -> p t r", t=2), ACT.Copy).then_inc(alt_ready, 1)
            act.wait_ge(zeroed, 2)
            for c in range(3):
                act.wait_ge(c_mm, c + 1)
                c_ps = (xr[2], xr[3], zp)[c][:, 0:256].rearrange("p (q a k) -> p q a k", a=2, k=K)
                for a in range(2):
                    if c < 2:
                        dst = c01[:, c].rearrange("p (q a) k -> p q a k", a=2)[:, :, a, 16 * a:16 * a + 16]
                        src = c_ps[:, :, a, :]
                    else:
                        dst = c2[64 * a:64 * a + 64, :, 16 * a:16 * a + 16]
                        src = c_ps[64 * a:64 * a + 64, :, a, :]
                    nc.scalar.activation(dst, src, ACT.Copy).then_inc(c_ready, 1)
            act.wait_ge(mlp_in, MLP)

            def step(i, u, last=False):
                s = 2 * i + u

                def filled(name):
                    k = scratch(name, last)[0]
                    if name == "eT":
                        act.wait_ge(e_read[u], i + 1 + ONE)
                    else:
                        act.wait_ge(sc_full[k], full_after(name, s, last))
                    return sc[k], sc_free[k]

                bank, free = filled("dense")
                nc.scalar.activation(dense_t[:], bank[0:D, 0:W], ACT.Copy).then_inc(free, 1)
                bank, free = filled("eT")
                nc.scalar.activation(e_t[:], bank[:].rearrange("p (a n) -> p a n", a=2), ACT.Copy).then_inc(free, 1)
                bank, free = filled("e01")
                act.wait_ge(mult[(PB - 1) % NXR], PER_XR * s + ONE)
                nc.scalar.activation(e_rep[:, 0:2, :], bank[:].rearrange("p (a n) -> p a n", a=2), ACT.Copy).then_inc(free, 1)
                bank, free = filled("e2")
                nc.scalar.activation(e_rep[:, 2, :], bank[:, 0:W], ACT.Copy).then_inc(free, 1)
                if not last:
                    hi(i + u, 1 - u)
                    mid(s + 1)
                act.wait_ge(contracted[1], s + 1 + ONE)
                nc.scalar.activation(z[:], zp[:].rearrange("p (a n) -> p a n", a=2), ACT.Copy).then_inc(z_ready, 1)
                for name in (USES_LAST if last else USES)[4:]:
                    bank, free = filled(name)
                    m = int(name[1]) if name != "y" else 0
                    if name[0] == "x":
                        nc.scalar.activation(x_t[:, 4 * m:4 * m + 4, :],
                                             bank[0:X3, :].bitcast(BF16).rearrange("p (h n) -> p h n", h=4),
                                             ACT.Copy).then_inc(free, 1)
                    elif name[0] == "a":
                        nc.scalar.activation(h1[:, m, :], bank[:, 0:W], ACT.Relu, bias=b1[:, m:m + 1]).then_inc(free, 1)
                    elif name[0] == "b":
                        nc.scalar.activation(h2[:, m, :], bank[:, 0:W], ACT.Relu, bias=b2[:, m:m + 1]).then_inc(free, 1)
                    else:
                        act.sem_inc(y_turn, 1)
                        nc.scalar.activation(y[:, bass.ts(s, W)], bank[0:1, 0:W], ACT.Copy).then_inc(free, 1)

            with act.Fori(0, PAIRS - 1) as i:
                step(i, 0)
                step(i, 1)
            step(PAIRS - 1, 0)
            step(PAIRS - 1, 1, last=True)
            act.wait_ge(sc_free[scratch("y", True)[0]], free_after("y", STEPS - 1, True))
            act.dma_start(out.rearrange("n o -> o n"), y[:]).then_inc(y_out, 16)
            act.wait_ge(y_out, 16)

        @block.vector
        def _(dve):
            def rest(i, u, s):
                dve.wait_ge(hi_done, s + 1)
                dve.wait_ge(x_loaded[u], 16 * i + 16)
                nc.vector.tensor_tensor(x_rest[:], x_in[u][:].rearrange("p j (f h) -> p j h f", h=H),
                                        x_parts[:, :, :, 0, :], ALU.subtract).then_inc(rest_done, 1)

            def low(u, s):
                dve.wait_ge(mid_done, s + 1)
                nc.vector.tensor_tensor(x_parts[:, :, :, 2, :], x_rest[:], x_parts[:, :, :, 1, :],
                                        ALU.subtract).then_inc(lo_done, 1)

            for k in range(NXR):
                dve.sem_inc(mult[k], ONE)
            nc.vector.memset(c01[:], 0.0).then_inc(zeroed, 1)
            nc.vector.memset(c2[:], 0.0).then_inc(zeroed, 1)
            rest(0, 0, 0)
            dve.wait_ge(const_in, 16)
            for c in range(3):
                dve.wait_ge(arow_ready, c + 1)
                if c > 0:
                    dve.wait_ge(al_ready, c)
                nc.vector.tensor_tensor(
                    al_terms[:].rearrange("p (k d) j -> p k d j", k=K),
                    alpha_rows[:, c, :].rearrange("p (j o k) -> p k o j", o=1, k=K).to_broadcast([P, K, D, 16]),
                    mask[:, c, :].rearrange("p (o j d) -> p o d j", o=1, d=D).to_broadcast([P, K, D, 16]),
                    ALU.mult).then_inc(al_step, 1)
                dve.wait_ge(al_step, c + 1)
                nc.vector.tensor_reduce(al[:, c, :], al_terms[:], AX.X, ALU.add).then_inc(al_ready, 1)
                if c == 0:
                    low(0, 0)
            dve.wait_ge(wts_in, WTS)
            for a in range(2):
                nc.vector.scalar_tensor_tensor(
                    out=w_diag[:, a].rearrange("p (h k) -> p h k", k=K),
                    in0=w_t[:, a].rearrange("p (h o) -> p h o", o=1).to_broadcast([P, H, K]), scalar=hv_t[:, a:a + 1],
                    in1=bd_mask[:, a:a + 1, :].to_broadcast([P, H, K]), op0=ALU.mult, op1=ALU.mult).then_inc(diag_ready, 1)

            def step(i, u, last=False):
                s = 2 * i + u
                for name in ("e01", "e2"):
                    dve.wait_ge(sc_free[scratch(name, last)[0]], free_after(name, s, last))
                for b in range(PB):
                    k, q = b % NXR, b // NXR
                    c = (b % 5) // 2
                    dve.wait_ge(xr_full[k], PER_XR * s + q + 1)
                    if b % HALF == 0:
                        dve.wait_ge(contracted[b // HALF], s + ONE)
                    nc.vector.tensor_tensor(prod[:, b, :].rearrange("p (a n) -> p a n", a=2),
                                            xr[k][:].rearrange("p (a n) -> p a n", a=2),
                                            e_rep[:, c:c + 1, :].to_broadcast([P, 2, W]), ALU.mult).then_inc(mult[k], 1)
                    if not last and b == 2:
                        rest(i + u, 1 - u, s + 1)
                    if not last and b == 10:
                        low(1 - u, s + 1)

            with dve.Fori(0, PAIRS - 1) as i:
                step(i, 0)
                step(i, 1)
            step(PAIRS - 1, 0)
            step(PAIRS - 1, 1, last=True)

        @block.tensor
        def _(pe):
            def xt(g, bank):
                for h in range(4):
                    for j in range(SUB):
                        ins = nc.tensor.transpose(bank[0:X3, :].bitcast(BF16)[:, (h * SUB + j) * P:(h * SUB + j + 1) * P],
                                                  x_parts[:, j, 4 * g + h].rearrange("p a f -> p (a f)"), ident_b[:])
                return ins

            for a in range(2):
                pe.sem_inc(e_read[a], ONE)
                pe.sem_inc(contracted[a], ONE)
            pe.wait_ge(const_in, 16)
            pe.wait_ge(wts_in, WTS)
            for c in range(3):
                nc.tensor.matmul(xr[c][:, 0:256], sel_x32[0:F, c, :], alpha_f[:], start=True, stop=True).then_inc(arow_mm, 1)
            pe.wait_ge(casts, 2)
            pe.wait_ge(lo_done, 1)
            for g in range(QUADS):
                if g >= NSC:
                    pe.wait_ge(sc_free[g % NSC], 1)
                xt(g, sc[g % NSC]).then_inc(sc_full[g % NSC], 1)
            for t in range(6):
                pe.wait_ge(al_ready, t // 2 + 1)
                pe.wait_ge(arow_ready, 3)
                ins = nc.tensor.transpose(xr[t // 4][:, (t % 4) * P:(t % 4 + 1) * P], al[:, t // 2, (t % 2) * P:(t % 2 + 1) * P], ident)
                if t % 4 == 3 or t == 5:
                    ins.then_inc(alt_mm, 1)
            pe.wait_ge(diag_ready, 2)
            for c in range(3):
                pe.wait_ge(alt_ready, 1 if c < 2 else 2)
                for a in range(2):
                    ins = nc.tensor.matmul((xr[2], xr[3], zp)[c][:, 0:256], al_t[:, 2 * c + a, :], w_diag[:, a, :], start=a == 0, stop=a == 1)
                ins.then_inc(c_mm, 1)
            pe.wait_ge(c_ready, 6)
            pe.wait_ge(alt_ready, 2)
            pe.wait_ge(mlp_in, MLP)

            def step(i, u, last=False):
                s = 2 * i + u

                def empty(name):
                    k = scratch(name, last)[0]
                    pe.wait_ge(sc_free[k], free_before(name, s, last))
                    return sc[k], e_read[u] if name == "eT" else sc_full[k]

                def freed(name):
                    pe.wait_ge(sc_free[scratch(name, last)[0]], free_after(name, s, last))

                def spread(b):
                    k, q = b % NXR, b // NXR
                    pe.wait_ge(mult[k], PER_XR * s + q + ONE)
                    h0, r = 4 * (b // 5), b % 5
                    if r < 4:
                        for a in range(2):
                            ins = nc.tensor.matmul(xr[k][:, a * W:(a + 1) * W], sel_x[0:X3, r // 2, :],
                                                   x_t[:, h0 + 2 * (r % 2) + a, :], start=True, stop=True)
                    else:
                        for a in range(2):
                            for hh in range(2):
                                ins = nc.tensor.matmul(xr[k][64 * hh:64 * hh + 64, a * W:(a + 1) * W], sel_x[0:X3, 2, 0:64],
                                                       x_t[:, h0 + 2 * a + hh, :], start=True, stop=True)
                    ins.then_inc(xr_full[k], 1)

                def contract(half):
                    for b in range(HALF * half + HALF - NXR, HALF * half + HALF):
                        pe.wait_ge(mult[b % NXR], PER_XR * s + b // NXR + 1 + ONE)
                    for m in range(5):
                        for q in range(4):
                            base, pp = 5 * (2 * half + q // 2), q % 2
                            pair = 4 * half + q
                            if m < 4:
                                c, a = m // 2, m % 2
                                lhs = c01[:, c, 2 * pair + a, :]
                                rhs = prod[:, base + 2 * c + pp, a * W:(a + 1) * W]
                            else:
                                lhs, rhs = c2[:, pair, :], prod[:, base + 4, pp * W:(pp + 1) * W]
                            ins = nc.tensor.matmul(zp[32 * q:32 * q + 32, half * W:(half + 1) * W], lhs, rhs,
                                                   start=m == 0, stop=m == 4)
                    ins.then_inc(contracted[half], 1)

                pe.wait_ge(gathered[u], 16 * SUB * NT * (i + 1))
                pe.wait_ge(dense_in[u], 16 * i + 16)
                bank, full = empty("dense")
                for j in range(SUB):
                    ins = nc.tensor.transpose(bank[0:D, j * P:(j + 1) * P], e_nat[u][:, j, NE:NE + D], ident)
                ins.then_inc(full, 1)
                bank, full = empty("eT")
                for a in range(2):
                    for j in range(SUB):
                        ins = nc.tensor.transpose(bank[:, (a * SUB + j) * P:(a * SUB + j + 1) * P], e_nat[u][:, j, a * P:(a + 1) * P], ident)
                ins.then_inc(full, 1)
                for k in range(NSC):
                    pe.wait_ge(sc_free[k], PER_SC * s + PRO[k])
                for b in range(NXR):
                    spread(b)
                freed("eT")
                bank, full = empty("e01")
                nc.tensor.matmul(bank[:, 0:W], sel_e[:, 0, :], e_t[:, 0, :], start=True, stop=True)
                nc.tensor.matmul(bank[:, W:2 * W], sel_e[:, 1, :], e_t[:, 0, :], start=True, stop=False)
                nc.tensor.matmul(bank[:, W:2 * W], sel_e[:, 2, :], e_t[:, 1, :], start=False, stop=True).then_inc(full, 1)
                bank, full = empty("e2")
                nc.tensor.matmul(bank[:, 0:W], sel_e[:, 3, :], e_t[:, 1, :], start=True, stop=True).then_inc(full, 1)
                for b in range(NXR, HALF):
                    spread(b)
                for b in range(HALF, HALF + NXR):
                    if b == HALF + 2:
                        pe.wait_ge(z_ready, s + ONE)
                        contract(0)
                    spread(b)
                for b in range(HALF + NXR, PB):
                    spread(b)
                contract(1)
                for name in (USES_LAST if last else USES)[4:]:
                    bank, full = empty(name)
                    m = int(name[1]) if name != "y" else 0
                    if name[0] == "x":
                        if m == 0:
                            pe.wait_ge(lo_done, s + 2)
                        ins = xt(m, bank)
                    elif name[0] == "a":
                        if m == 0:
                            freed("dense")
                        sl = slice(m * P, (m + 1) * P)
                        nc.tensor.matmul(bank[:, 0:W], w1d[:, sl], dense_t[:], start=True, stop=False)
                        if m == 0:
                            pe.wait_ge(z_ready, s + 1 + ONE)
                        for a in range(2):
                            ins = nc.tensor.matmul(bank[:, 0:W], w1[:, a, sl], z[:, a, :], start=False, stop=a == 1)
                    elif name[0] == "b":
                        for c in range(N1 // P):
                            if m == 0:
                                freed(f"a{c}")
                            ins = nc.tensor.matmul(bank[:, 0:W], w2[:, c, m * P:(m + 1) * P], h1[:, c, :], start=c == 0, stop=c == N1 // P - 1)
                    else:
                        for c in range(N2 // P):
                            freed(f"b{c}")
                            ins = nc.tensor.matmul(bank[0:1, 0:W], w3[:, c:c + 1], h2[:, c, :], start=c == 0, stop=c == N2 // P - 1)
                    ins.then_inc(full, 1)

            with pe.Fori(0, PAIRS - 1) as i:
                step(i, 0)
                step(i, 1)
            step(PAIRS - 1, 0)
            step(PAIRS - 1, 1, last=True)


def shape_constants():
    import numpy as np
    start = [min((NE * f) // F, NE - NW) for f in range(F)]
    con = np.zeros((P, C_END), np.float32)
    con[:, C_ID:C_ID + P] = np.eye(P)
    sel_e = con[:, C_SE:C_SE + 4 * P].reshape(P, 4, P)
    sel_x = con[:, C_SX:C_SX + 3 * P].reshape(P, 3, P)
    mask = con[:, C_MK:C_MK + 3 * 256].reshape(P, 3, 256)
    bd = con[:, C_BD:C_BD + 32].reshape(P, 2, 16)
    for f in range(F):
        c = f // 16
        for row0 in ([8 * (f - 16 * c)] if c < 2 else [8 * (f - 32), 64 + 8 * (f - 32)]):
            for i in range(NW):
                row, at = row0 + i, start[f] + i
                for part in range(3):
                    sel_x[part * F + f, c, row] = 1
                for t, (cc, a) in enumerate(SE_TERMS):
                    if cc == c and a == at // P:
                        sel_e[at - a * P, t, row] = 1
                q = np.arange(256)
                mask[row, c] = (256 * f + q) // F == at
    for p in range(P):
        for a in range(2):
            bd[p, a, 8 * a + p // 16] = 1
    return con


def kernel(**inputs):
    import numpy as _np
    import concourse.bacc as _bacc
    from concourse.bass_utils import run_bass_kernel_spmd as _run

    nc = _bacc.Bacc("TRN2", target_bir_lowering=False, num_devices=1)
    arrays, T = {}, {}
    for name in list(inputs) + ["const"]:
        a = shape_constants() if name == "const" else _np.ascontiguousarray(inputs[name])
        arrays[f"in_{name}_dram"] = a
        T[name] = nc.dram_tensor(f"in_{name}_dram", a.shape, mybir.dt.from_np(a.dtype), kind="ExternalInput").ap()
    out = nc.dram_tensor("out_0_dram", (B, 1), F32, kind="ExternalOutput").ap()
    interaction_tower(nc, T, out)
    r = _run(nc, [arrays], core_ids=[0])
    return r.results[0]["out_0_dram"]
```

```python
import concourse.bass as bass
from concourse import mybir
from contextlib import ExitStack

F32 = mybir.dt.float32
BF16 = mybir.dt.bfloat16
I32 = mybir.dt.int32
F16 = mybir.dt.float16
ALU = mybir.AluOpType
ACT = mybir.ActivationFunctionType
AX = mybir.AxisListType

P = 128
B = 2048
NT, D = 16, 16
NE = NT * D
F, H, K = 39, 16, 16
NW = 8
N1, N2 = 512, 256
SUB = 2
W = SUB * P
STEPS = B // W
LOOPS = (STEPS - 2) // 2
NXR, NSC = 5, 2
NOH = 4
QUADS = H // 4
PB = 5 * QUADS
HALF = PB // 2
X3 = 3 * F

VOCAB = [1000, 1250, 125000, 12500, 1250, 1250, 12500, 125000, 12500, 1000, 125000, 12500, 12500, 125000, 125000, 1000]
DENSE_PAIRS = [(0, 1), (9, 15)]
DENSE = [t for pair in DENSE_PAIRS for t in pair]
NPAIR, NDENSE = len(DENSE_PAIRS), len(DENSE)
GATHERED = [t for t in range(NT) if t not in DENSE]
NG = len(GATHERED) * D
VP = 125
CHUNKS = {t: VOCAB[t] // VP for t in DENSE}
CHUNK0 = {t: sum(CHUNKS[v] for v in DENSE[:n]) for n, t in enumerate(DENSE)}
NCH = sum(CHUNKS.values())
NA = 5
WINDOW = [min((NE * f) // F, NE - NW) for f in range(F)]


def meets(tables):
    return [c for c in range(3) if any((WINDOW[f] + i) // D in tables for f in range(16 * c, min(16 * c + 16, F)) for i in range(NW))]


E_TERMS = [(c, a) for c in range(3) for a in range(2) if c in meets(GATHERED[8 * a:8 * a + 8])]
OH_TERMS = [(c, n) for c in range(3) for n in range(NPAIR) if c in meets(DENSE_PAIRS[n])]
NET, NOT = len(E_TERMS), len(OH_TERMS)

C_ID, C_SE, C_BD, C_ROW = 0, P, P + NET * P, P + NET * P + 32
C_END = C_ROW + NCH
B_SX, B_SO, B_ID, B_MD = 0, 3 * P, (3 + NOT) * P, (4 + NOT) * P
B_END = B_MD + NA * D * 64


def interaction_tower(nc, T, out):
    with ExitStack() as ctx:
        def sb(name, shape, dt=F32):
            return ctx.enter_context(nc.sbuf_tensor(name, shape, dt))

        def sem(name):
            return ctx.enter_context(nc.semaphore(name))

        const = sb("const", [P, C_END])
        ident = const[:, C_ID:C_ID + P]
        sel_e = const[:, C_SE:C_SE + NET * P].rearrange("p (t r) -> p t r", t=NET)
        bd_mask = const[:, C_BD:C_BD + 32].rearrange("p (a k) -> p a k", a=2)
        vocab_row = const[:, C_ROW:C_ROW + NCH]
        const_b = sb("const_b", [P, B_END], BF16)
        sel_x = const_b[:, B_SX:B_SX + 3 * P].rearrange("p (c r) -> p c r", c=3)
        ident_b = const_b[:, B_ID:B_ID + P]
        sel_o = const_b[:, B_SO:B_SO + NOT * P].rearrange("p (t r) -> p t r", t=NOT)
        sel_a = const_b[:, B_MD:].rearrange("p (m d r) -> p m d r", m=NA, d=D)
        small = sb("small", [P, NA + NCH, D])
        small_rest = sb("small_rest", [P, NA + NCH, D])
        small_parts = sb("small_parts", [P, NA + NCH, 4, D], BF16)
        idx_flat = sb("idx_flat", [P, NDENSE * B // P], I32)
        idx_flat16 = sb("idx_flat16", [P, NDENSE * B // P], F16)
        idx = sb("idx", [VP, NDENSE, B], F16)
        onehot = [sb(f"onehot{n}", [VP, B], BF16) for n in range(NOH)]
        oh_t = sb("oh_t", [P, NPAIR, B], BF16)
        oh_now = sb("oh_now", [P, NPAIR, W], BF16)
        al = sb("al", [P, 3, 256])
        al_t = sb("al_t", [P, 6, P])
        w_t = sb("w_t", [P, 2, H])
        hv_t = sb("hv_t", [P, 2])
        w_diag = sb("w_diag", [P, 2, H * K])
        c01 = sb("c01", [P, 2, H, 32])
        c2 = sb("c2", [P, H // 2, 32])
        w1 = sb("w1", [P, 2, N1])
        w1d = sb("w1d", [D, N1])
        w2 = sb("w2", [P, N1 // P, N2])
        w3 = sb("w3", [P, N2 // P])
        b1 = sb("b1", [P, N1 // P])
        b2 = sb("b2", [P, N2 // P])
        ids = [sb(f"ids{u}", [P, SUB, NT], I32) for u in range(2)]
        x_in = [sb(f"x_in{u}", [P, SUB, F * H]) for u in range(2)]
        e_nat = [sb(f"e_nat{u}", [P, SUB, NE]) for u in range(2)]
        x_parts = sb("x_parts", [P, SUB, H, X3], BF16)
        x_part = [x_parts[:, :, :, n * F:(n + 1) * F] for n in range(3)]
        x_rest = sb("x_rest", [P, SUB, H, F])
        x_t = [sb(f"x_t{u}", [X3, H, W], BF16) for u in range(2)]
        e_t = sb("e_t", [P, 2, W])
        dense_all = sb("dense_all", [D, B])
        dense_t = sb("dense_t", [D, W])
        e_rep = [sb(f"e_rep{u}", [P, 3, W]) for u in range(2)]
        prod = sb("prod", [P, PB, 2 * W])
        z = sb("z", [P, 2, W])
        h1 = sb("h1", [P, N1 // P, W])
        h2 = sb("h2", [P, N2 // P, W])
        y = sb("y", [1, B])

        xr = [ctx.enter_context(nc.psum_tensor(f"xr{k}", [P, 512], F32)) for k in range(NXR)]
        sc = [ctx.enter_context(nc.psum_tensor(f"sc{k}", [P, 512], F32)) for k in range(NSC)]
        zp = ctx.enter_context(nc.psum_tensor("zp", [P, 512], F32))

        const_in, wts_in, mlp_in = sem("const_in"), sem("wts_in"), sem("mlp_in")
        ids_in = [sem(f"ids_in{u}") for u in range(2)]
        x_loaded = [sem(f"x_loaded{u}") for u in range(2)]
        gathered = [sem(f"gathered{u}") for u in range(2)]
        e_read = [sem(f"e_read{u}") for u in range(2)]
        y_out = sem("y_out")
        y_turn = sem("y_turn")
        turn = sem("turn")
        small_in, idx_in, idx_cast, idx_out, idx_all = (sem(n) for n in ("small_in", "idx_in", "idx_cast", "idx_out", "idx_all"))
        const_b_in = sem("const_b_in")
        small_hi, small_left, small_mid, small_lo = (sem(n) for n in ("small_hi", "small_left", "small_mid", "small_lo"))
        oh_ready = [sem(f"oh_ready{n}") for n in range(NOH)]
        oh_read = [sem(f"oh_read{n}") for n in range(NOH)]
        oh_kept = sem("oh_kept")
        oh_now_ready = sem("oh_now_ready")
        dense_ready = sem("dense_ready")
        zeroed = sem("zeroed")
        diag_ready = sem("diag_ready")
        al_mm, al_ready = sem("al_mm"), sem("al_ready")
        alt_mm, alt_ready = sem("alt_mm"), sem("alt_ready")
        c_mm, c_ready = sem("c_mm"), sem("c_ready")
        hi_done, rest_done, mid_done, lo_done = sem("hi_done"), sem("rest_done"), sem("mid_done"), sem("lo_done")
        sc_full = [sem(f"sc_full{k}") for k in range(NSC)]
        sc_free = [sem(f"sc_free{k}") for k in range(NSC)]
        xr_full = [sem(f"xr_full{k}") for k in range(NXR)]
        mult = [sem(f"mult{k}") for k in range(NXR)]
        contracted = [sem(f"contracted{a}") for a in range(2)]
        z_ready = sem("z_ready")

        ONE = 1

        MLP_USES = ["a0", "a1", "a2", "a3", "b0", "b1", "y"]
        NEXT_USES = ["x0", "x1", "x2", "x3", "eT", "e01", "e2"]
        ORDER = {"pro": NEXT_USES, "first": NEXT_USES, "mid": MLP_USES + NEXT_USES, "last": MLP_USES, "end": MLP_USES}
        PER_STEP = len(ORDER["mid"])
        assert PER_STEP % NSC == 0 and PB % NXR == 0
        PER_XR = PB // NXR
        AT = {"pro": 0, "first": len(NEXT_USES), "mid": 0, "last": PER_STEP * (STEPS - 1), "end": PER_STEP * (STEPS - 1) + len(MLP_USES)}
        assert PER_STEP == 2 * len(NEXT_USES)

        def scratch(name, phase, s):
            n = AT[phase] + ORDER[phase].index(name)
            return n % NSC, n // NSC + (PER_STEP // NSC * s if phase == "mid" else 0)

        OH_ORDER = [(t, c) for pair in DENSE_PAIRS for c in range(max(CHUNKS[t] for t in pair)) for t in pair if c < CHUNKS[t]]

        x_dram = T["r_x0"].rearrange("(s j p) f h -> p s j (f h)", p=P, j=SUB)
        ids_dram = T["ids"].rearrange("(s j p) t -> p s j t", p=P, j=SUB)

        idx_dram = nc.dram_tensor("idx16", [NDENSE, B], F16, kind="Internal").ap()

        block = ctx.enter_context(nc.Block())

        @block.sync
        def _(sp):
            def load_ids(s, u):
                sp.dma_start(ids[u][:], ids_dram[:, bass.ds(s, 1)].rearrange("p o j t -> p (o j) t")).then_inc(ids_in[u], 16)

            def load_x(s, u):
                sp.dma_start(x_in[u][:], x_dram[:, bass.ds(s, 1)].rearrange("p o j c -> p (o j) c")).then_inc(x_loaded[u], 16)

            load_ids(0, 0)
            for n, t in enumerate(DENSE):
                sp.dma_start(idx_flat[n * 32:n * 32 + 32, :], T["ids_t"][t].rearrange("(a n) -> a n", a=32)).then_inc(idx_in, 16)
            load_x(0, 0)
            sp.wait_ge(zeroed, 1)
            sp.dma_start(small[:, 0:NA - 1, :], T["L0_rec_alpha"][0:(NA - 1) * P].rearrange("(m p) k -> p m k", p=P)).then_inc(small_in, 16)
            sp.dma_start(small[0:F * 16 - (NA - 1) * P, NA - 1, :], T["L0_rec_alpha"][(NA - 1) * P:]).then_inc(small_in, 16)
            for t in DENSE:
                sp.dma_start(small[0:VP, NA + CHUNK0[t]:NA + CHUNK0[t] + CHUNKS[t], :],
                             T[f"tbl_{t}"].rearrange("(p c) d -> p c d", p=VP)).then_inc(small_in, 16)
            sp.dma_start(const[:], T["const"]).then_inc(const_in, 16)
            sp.wait_ge(idx_out, 16)
            sp.dma_start(idx[:].rearrange("p t n -> p (t n)"),
                         idx_dram.rearrange("(o t) n -> o (t n)", o=1).to_broadcast([VP, NDENSE * B])).then_inc(idx_all, 16)
            sp.dma_start(const_b[:], T["const_b"]).then_inc(const_b_in, 16)
            load_ids(1, 1)
            load_x(1, 1)
            w1_dram = T["W_top1"][0:NE].rearrange("(k a h) n -> h k a n", a=2, h=8)
            for hh in range(8):
                sp.dma_start(w1[16 * hh:16 * hh + 16], w1_dram[hh]).then_inc(mlp_in, 16)
            sp.dma_start(w1d[:], T["W_top1"][NE:NE + D]).then_inc(mlp_in, 16)
            sp.dma_start(w2[:], T["W_top2"].rearrange("(c p) n -> p c n", p=P)).then_inc(mlp_in, 16)
            sp.dma_start(dense_all[:], T["dense_ctx_t"]).then_inc(mlp_in, 16)

            def ahead(i, u):
                s = 2 * i + u
                sp.wait_ge(gathered[u], 16 * SUB * len(GATHERED) * (i + 1))
                load_ids(s + 2, u)
                sp.wait_ge(rest_done, s + 1)
                load_x(s + 2, u)

            with sp.Fori(0, STEPS // 2 - 1) as i:
                ahead(i, 0)
                ahead(i, 1)
        WTS, MLP, SMALL = 16 * 17, 16 * 14, 16 * (2 + NDENSE)

        @block.gpsimd
        def _(pool):
            with pool.Fori(0, STEPS // 2) as i:
                for u in range(2):
                    pool.wait_ge(ids_in[u], 16 * i + 16)
                    pool.wait_ge(e_read[u], i + ONE)
                    pool.sem_inc(turn, 1)
                    for j in range(SUB):
                        for n, t in enumerate(GATHERED):
                            nc.gpsimd.indirect_dma_start(
                                e_nat[u][:, j, n * D:(n + 1) * D], None, T[f"tbl_{t}"],
                                bass.IndirectOffsetOnAxis(ap=ids[u][:, j, t:t + 1], axis=0)).then_inc(gathered[u], 16)

        @block.scalar
        def _(act):
            def hi(i, u):
                act.wait_ge(x_loaded[u], 16 * i + 16)
                nc.scalar.activation(x_part[0], x_in[u][:].rearrange("p j (f h) -> p j h f", h=H),
                                     ACT.Copy).then_inc(hi_done, 1)

            def mid(s):
                act.wait_ge(rest_done, s + 1)
                nc.scalar.activation(x_part[1], x_rest[:], ACT.Copy).then_inc(mid_done, 1)

            act.sem_inc(z_ready, ONE)
            act.wait_ge(idx_cast, 1)
            act.dma_start(idx_dram.rearrange("t (a n) -> (t a) n", a=32), idx_flat16[:]).then_inc(idx_out, 16)
            with nc.allow_non_contiguous_dma(reason="w, hv and biases go to partitions element by element, once"):
                for a in range(2):
                    for kk in range(8):
                        act.dma_start(w_t[16 * kk:16 * kk + 16, a, :],
                                      T["L0_rec_w"][8 * a + kk].rearrange("h d -> d h")).then_inc(wts_in, 16)
                act.dma_start(hv_t[:], T["L0_rec_hv"].rearrange("(a k) d o -> (k d) (a o)", a=2)).then_inc(wts_in, 16)
                act.dma_start(b1[:], T["b_top1"].rearrange("(m p) -> p m", p=P)).then_inc(mlp_in, 16)
                act.dma_start(b2[:], T["b_top2"].rearrange("(m p) -> p m", p=P)).then_inc(mlp_in, 16)
                act.dma_start(w3[:], T["W_top3"].rearrange("(m p) o -> p (m o)", p=P)).then_inc(mlp_in, 16)
            hi(0, 0)
            act.wait_ge(small_in, SMALL)
            act.wait_ge(zeroed, 4)
            nc.scalar.activation(small_parts[:, :, 0, :], small[:], ACT.Copy).then_inc(small_hi, 1)
            mid(0)
            act.wait_ge(small_left, 1)
            nc.scalar.activation(small_parts[:, :, 1, :], small_rest[:], ACT.Copy).then_inc(small_mid, 1)
            act.wait_ge(al_mm, 1)
            nc.scalar.activation(al[:, 0:2, :], zp[:].rearrange("p (c q) -> p c q", c=2), ACT.Copy).then_inc(al_ready, 1)
            act.wait_ge(al_mm, 2)
            nc.scalar.activation(al[:, 2, :], xr[4][:, 0:256], ACT.Copy).then_inc(al_ready, 1)
            for n in range(2):
                act.wait_ge(alt_mm, n + 1)
                t0, t1 = (0, 4) if n == 0 else (4, 6)
                nc.scalar.activation(al_t[:, t0:t1, :], sc[n][:, 0:(t1 - t0) * P].rearrange("p (t r) -> p t r", t=t1 - t0),
                                     ACT.Copy).then_inc(alt_ready, 1)
            act.wait_ge(c_mm, 3)
            for c in range(3):
                c_ps = (zp[:, 0:256], zp[:, 256:512], xr[4][:, 0:256])[c].rearrange("p (q a k) -> p q a k", a=2, k=K)
                for a in range(2):
                    if c < 2:
                        dst = c01[:, c].rearrange("p (q a) k -> p q a k", a=2)[:, :, a, 16 * a:16 * a + 16]
                        src = c_ps[:, :, a, :]
                    else:
                        dst = c2[64 * a:64 * a + 64, :, 16 * a:16 * a + 16]
                        src = c_ps[64 * a:64 * a + 64, :, a, :]
                    nc.scalar.activation(dst, src, ACT.Copy).then_inc(c_ready, 1)
            for n in range(NPAIR):
                last = max(k for k in range(NCH) if OH_ORDER[k][0] in DENSE_PAIRS[n])
                act.wait_ge(oh_read[last % NOH], last // NOH + 1)
                for g in range(4):
                    nc.scalar.activation(oh_t[:, n, g * 512:(g + 1) * 512], xr[g][:], ACT.Copy).then_inc(oh_kept, 1)
            act.wait_ge(mlp_in, MLP)

            def dense_slice(s):
                nc.scalar.activation(dense_t[:], dense_all[:, bass.ts(s, W)], ACT.Copy).then_inc(dense_ready, 1)

            def empty(name, phase, s, u):
                k, before = scratch(name, phase, s)
                bank, free, m = sc[k], sc_free[k], int(name[1]) if name[0] in "abx" else 0
                act.wait_ge(sc_full[k], before + 1)
                if name == "eT":
                    act.sem_inc(e_read[u], 1)
                    nc.scalar.activation(e_t[:], bank[:].rearrange("p (a n) -> p a n", a=2), ACT.Copy).then_inc(free, 1)
                    after = {"pro": 0, "first": 1, "mid": s + 1}[phase]
                    nc.scalar.activation(oh_now[:], oh_t[:, :, bass.ts(after, W)], ACT.Copy).then_inc(oh_now_ready, 1)
                elif name == "e01":
                    nc.scalar.activation(e_rep[u][:, 0:2, :], bank[:].rearrange("p (a n) -> p a n", a=2), ACT.Copy).then_inc(free, 1)
                elif name == "e2":
                    nc.scalar.activation(e_rep[u][:, 2, :], bank[:, 0:W], ACT.Copy).then_inc(free, 1)
                elif name[0] == "x":
                    nc.scalar.activation(x_t[u][:, 4 * m:4 * m + 4, :], bank[0:X3, :].bitcast(BF16).rearrange("p (h n) -> p h n", h=4),
                                         ACT.Copy).then_inc(free, 1)
                elif name[0] == "a":
                    nc.scalar.activation(h1[:, m, :], bank[:, 0:W], ACT.Relu, bias=b1[:, m:m + 1]).then_inc(free, 1)
                elif name[0] == "b":
                    nc.scalar.activation(h2[:, m, :], bank[:, 0:W], ACT.Relu, bias=b2[:, m:m + 1]).then_inc(free, 1)
                else:
                    act.sem_inc(y_turn, 1)
                    done = {"mid": s - 1, "last": STEPS - 2, "end": STEPS - 1}[phase]
                    nc.scalar.activation(y[:, bass.ts(done, W)], bank[0:1, 0:W], ACT.Copy).then_inc(free, 1)

            def step(i, s, u, phase):
                if phase != "last":
                    hi(i, 1 - u)
                for name in ORDER[phase]:
                    if name == "a2" or name == "x0" and phase == "first":
                        if phase != "last":
                            mid(s + 1)
                    if name == "e01":
                        act.wait_ge(contracted[1], s + 1 + ONE)
                        nc.scalar.activation(z[:], zp[:].rearrange("p (a n) -> p a n", a=2), ACT.Copy).then_inc(z_ready, 1)
                        act.wait_ge(mult[(PB - 1) % NXR], PER_XR * s + ONE)
                    empty(name, phase, s, 1 - u)
                    if name == "a3":
                        dense_slice(s)
                if phase == "first":
                    dense_slice(s)
                if phase == "last":
                    act.wait_ge(contracted[1], s + 1 + ONE)
                    nc.scalar.activation(z[:], zp[:].rearrange("p (a n) -> p a n", a=2), ACT.Copy).then_inc(z_ready, 1)

            for name in ORDER["pro"]:
                empty(name, "pro", 0, 0)
            step(0, 0, 0, "first")
            with act.Fori(0, LOOPS) as i:
                step(i + 1, 2 * i + 1, 1, "mid")
                step(i + 1, 2 * i + 2, 0, "mid")
            step(0, STEPS - 1, 1, "last")
            for name in ORDER["end"]:
                empty(name, "end", 0, 0)
            k, before = scratch("y", "end", 0)
            act.wait_ge(sc_free[k], before + 1)
            act.dma_start(out.rearrange("n o -> o n"), y[:]).then_inc(y_out, 16)
            act.wait_ge(y_out, 16)

        @block.vector
        def _(dve):
            def rest(i, u, s):
                dve.wait_ge(hi_done, s + 1)
                dve.wait_ge(x_loaded[u], 16 * i + 16)
                nc.vector.tensor_tensor(x_rest[:], x_in[u][:].rearrange("p j (f h) -> p j h f", h=H),
                                        x_part[0], ALU.subtract).then_inc(rest_done, 1)

            def low(u, s):
                dve.wait_ge(mid_done, s + 1)
                nc.vector.tensor_tensor(x_part[2], x_rest[:], x_part[1],
                                        ALU.subtract).then_inc(lo_done, 1)

            def diagonal():
                dve.wait_ge(wts_in, WTS)
                dve.wait_ge(const_in, 16)
                for a in range(2):
                    nc.vector.scalar_tensor_tensor(
                        out=w_diag[:, a].rearrange("p (h k) -> p h k", k=K),
                        in0=w_t[:, a].rearrange("p (h o) -> p h o", o=1).to_broadcast([P, H, K]), scalar=hv_t[:, a:a + 1],
                        in1=bd_mask[:, a:a + 1, :].to_broadcast([P, H, K]), op0=ALU.mult, op1=ALU.mult).then_inc(diag_ready, 1)

            for k in range(NXR):
                dve.sem_inc(mult[k], ONE)
            nc.vector.memset(small[:], 0.0).then_inc(zeroed, 1)
            nc.vector.memset(c01[:], 0.0).then_inc(zeroed, 1)
            nc.vector.memset(c2[:], 0.0).then_inc(zeroed, 1)
            nc.vector.memset(small_parts[:, :, 3, :], 0.0).then_inc(zeroed, 1)
            dve.wait_ge(idx_in, 16 * NDENSE)
            nc.vector.tensor_copy(idx_flat16[:], idx_flat[:]).then_inc(idx_cast, 1)
            for u in range(2):
                nc.vector.memset(e_nat[u][:, :, NG:], 0.0).then_inc(zeroed, 1)
            rest(0, 0, 0)
            low(0, 0)
            dve.wait_ge(small_hi, 1)
            nc.vector.tensor_tensor(small_rest[:], small[:], small_parts[:, :, 0, :], ALU.subtract).then_inc(small_left, 1)
            dve.wait_ge(small_mid, 1)
            nc.vector.tensor_tensor(small_parts[:, :, 2, :], small_rest[:], small_parts[:, :, 1, :], ALU.subtract).then_inc(small_lo, 1)
            dve.wait_ge(idx_all, 16)
            dve.wait_ge(const_in, 16)
            for n, (t, c) in enumerate(OH_ORDER):
                if n >= NOH:
                    dve.wait_ge(oh_read[n % NOH], n // NOH)
                row = CHUNK0[t] + c
                nc.vector.tensor_scalar(onehot[n % NOH][:], idx[:, DENSE.index(t), :], vocab_row[0:VP, row:row + 1], None,
                                        ALU.is_equal).then_inc(oh_ready[n % NOH], 1)
                if n == 3:
                    diagonal()

            def step(i, s, u, phase):
                for name in ("e01", "e2"):
                    k, before = scratch(name, "pro", 0) if phase == "first" else scratch(name, "mid", s - 1)
                    dve.wait_ge(sc_free[k], before + 1)
                for b in range(PB):
                    k, q = b % NXR, b // NXR
                    c = (b % 5) // 2
                    dve.wait_ge(xr_full[k], PER_XR * s + q + 1)
                    if b % HALF == 0:
                        dve.wait_ge(contracted[b // HALF], s + ONE)
                    nc.vector.tensor_tensor(prod[:, b, :].rearrange("p (a n) -> p a n", a=2),
                                            xr[k][:].rearrange("p (a n) -> p a n", a=2),
                                            e_rep[u][:, c:c + 1, :].to_broadcast([P, 2, W]), ALU.mult).then_inc(mult[k], 1)
                    if b == 1 and phase != "last":
                        rest(i, 1 - u, s + 1)
                    if b == 6 and phase != "last":
                        low(1 - u, s + 1)

            step(0, 0, 0, "first")
            with dve.Fori(0, LOOPS) as i:
                step(i + 1, 2 * i + 1, 1, "mid")
                step(i + 1, 2 * i + 2, 0, "mid")
            step(0, STEPS - 1, 1, "last")

        @block.tensor
        def _(pe):
            def fill(name, phase, s):
                k, before = scratch(name, phase, s)
                if not (phase == "pro" and before == 0):
                    pe.wait_ge(sc_free[k], before)
                return sc[k], sc_full[k]

            def emptied(name, phase, s):
                k, before = scratch(name, phase, s)
                pe.wait_ge(sc_free[k], before + 1)

            def transpose_x(g, phase, s):
                bank, full = fill(f"x{g}", phase, s)
                for h in range(4):
                    for j in range(SUB):
                        ins = nc.tensor.transpose(bank[0:X3, :].bitcast(BF16)[:, (h * SUB + j) * P:(h * SUB + j + 1) * P],
                                                  x_parts[:, j, 4 * g + h], ident_b)
                ins.then_inc(full, 1)

            def transpose_e(phase, s, u, count):
                pe.wait_ge(gathered[u], 16 * SUB * len(GATHERED) * count)
                bank, full = fill("eT", phase, s)
                for a in range(2):
                    for j in range(SUB):
                        ins = nc.tensor.transpose(bank[:, (a * SUB + j) * P:(a * SUB + j + 1) * P], e_nat[u][:, j, a * P:(a + 1) * P], ident)
                ins.then_inc(full, 1)

            def spread_e(phase, s):
                emptied("eT", phase, s)
                pe.wait_ge(oh_now_ready, {"pro": 1, "first": 2, "mid": s + 2}[phase])
                for name, chunks in (("e01", (0, 1)), ("e2", (2,))):
                    bank, full = fill(name, phase, s)
                    for c in chunks:
                        terms = [(sel_e[:, n, :], e_t[:, a, :]) for n, (cc, a) in enumerate(E_TERMS) if cc == c]
                        terms += [(sel_o[:, n, :], oh_now[:, a, :]) for n, (cc, a) in enumerate(OH_TERMS) if cc == c]
                        for n, (sel, e) in enumerate(terms):
                            ins = nc.tensor.matmul(bank[:, (c % 2) * W:(c % 2 + 1) * W], sel, e, start=n == 0, stop=n == len(terms) - 1)
                    ins.then_inc(full, 1)

            def spread_x(b, s, u, phase):
                k, q = b % NXR, b // NXR
                if b % 5 == 0:
                    emptied(f"x{b // 5}", *(("pro", 0) if phase == "first" else ("mid", s - 1)))
                pe.wait_ge(mult[k], PER_XR * s + q + ONE)
                h0, r = 4 * (b // 5), b % 5
                if r < 4:
                    h = h0 + 2 * (r % 2)
                    ins = nc.tensor.matmul(xr[k][:], sel_x[0:X3, r // 2, :], x_t[u][0:X3, h:h + 2, :], start=True, stop=True)
                else:
                    for hh in range(2):
                        ins = nc.tensor.matmul(xr[k][64 * hh:64 * hh + 64, :], sel_x[0:X3, 2, 0:64],
                                               x_t[u][0:X3, h0 + hh:h0 + 4:2, :], start=True, stop=True)
                ins.then_inc(xr_full[k], 1)

            def contract(half, s):
                for b in range(HALF * half + HALF - NXR, HALF * half + HALF):
                    pe.wait_ge(mult[b % NXR], PER_XR * s + b // NXR + 1 + ONE)
                if half == 0:
                    pe.wait_ge(z_ready, s + ONE)
                for m in range(5):
                    for q in range(4):
                        base, pp = 5 * (2 * half + q // 2), q % 2
                        pair = 4 * half + q
                        if m < 4:
                            c, a = m // 2, m % 2
                            lhs = c01[:, c, 2 * pair + a, :]
                            rhs = prod[:, base + 2 * c + pp, a * W:(a + 1) * W]
                        else:
                            lhs, rhs = c2[:, pair, :], prod[:, base + 4, pp * W:(pp + 1) * W]
                        ins = nc.tensor.matmul(zp[32 * q:32 * q + 32, half * W:(half + 1) * W], lhs, rhs,
                                               start=m == 0, stop=m == 4)
                ins.then_inc(contracted[half], 1)

            def mlp(name, phase, s, done):
                bank, full = fill(name, phase, s)
                m = int(name[1]) if name != "y" else 0
                if name[0] == "a":
                    cols = slice(m * P, (m + 1) * P)
                    pe.wait_ge(dense_ready, done + 1)
                    nc.tensor.matmul(bank[:, 0:W], w1d[:, cols], dense_t[:], start=True, stop=False)
                    pe.wait_ge(z_ready, done + 1 + ONE)
                    for a in range(2):
                        ins = nc.tensor.matmul(bank[:, 0:W], w1[:, a, cols], z[:, a, :], start=False, stop=a == 1)
                elif name[0] == "b":
                    for c in range(N1 // P):
                        emptied(f"a{c}", phase, s)
                        ins = nc.tensor.matmul(bank[:, 0:W], w2[:, c, m * P:(m + 1) * P], h1[:, c, :], start=c == 0, stop=c == N1 // P - 1)
                else:
                    for c in range(N2 // P):
                        emptied(f"b{c}", phase, s)
                        ins = nc.tensor.matmul(bank[0:1, 0:W], w3[:, c:c + 1], h2[:, c, :], start=c == 0, stop=c == N2 // P - 1)
                ins.then_inc(full, 1)

            for a in range(2):
                pe.sem_inc(e_read[a], ONE)
                pe.sem_inc(contracted[a], ONE)
            pe.wait_ge(const_b_in, 16)
            pe.wait_ge(small_lo, 1)
            for c in range(3):
                al_ps = (zp[:, 0:256], zp[:, 256:512], xr[4][:, 0:256])[c].rearrange("p (k d) -> p k d", k=K)
                for d in range(D):
                    for part in range(3):
                        for tile in range(2):
                            m = 2 * c + tile if c < 2 else NA - 1
                            rows = min(P, F * 16 - m * P)
                            ins = nc.tensor.matmul(al_ps[64 * tile:64 * tile + 64, :, d], sel_a[0:rows, m, d, :],
                                                   small_parts[0:rows, m, part, :], start=part == 0, stop=part == 2)
                if c > 0:
                    ins.then_inc(al_mm, 1)

            def lookup(n0, n1):
                for n in range(n0, n1):
                    t, c = OH_ORDER[n]
                    pair = DENSE.index(t) // 2
                    side = DENSE.index(t) % 2
                    pe.wait_ge(oh_ready[n % NOH], n // NOH + 1)
                    if pair > 0 and c == 0:
                        pe.wait_ge(oh_kept, 4 * pair)
                    for g in range(4):
                        ins = nc.tensor.matmul(xr[g][64 * side:64 * side + 64, :], small_parts[0:VP, NA + CHUNK0[t] + c].rearrange("p a d -> p (a d)"),
                                               onehot[n % NOH][:, g * 512:(g + 1) * 512], start=c == 0, stop=c == CHUNKS[t] - 1)
                    ins.then_inc(oh_read[n % NOH], 1)

            lookup(0, 4)
            pe.wait_ge(const_in, 16)
            for t in range(6):
                pe.wait_ge(al_ready, 1 if t < 4 else 2)
                ins = nc.tensor.transpose(sc[t // 4][:, (t % 4) * P:(t % 4 + 1) * P], al[:, t // 2, (t % 2) * P:(t % 2 + 1) * P], ident)
                if t % 4 == 3 or t == 5:
                    ins.then_inc(alt_mm, 1)
            pe.wait_ge(diag_ready, 2)
            for c in range(3):
                pe.wait_ge(alt_ready, 1 if c < 2 else 2)
                for a in range(2):
                    ins = nc.tensor.matmul((zp[:, 0:256], zp[:, 256:512], xr[4][:, 0:256])[c], al_t[:, 2 * c + a, :], w_diag[:, a, :],
                                           start=a == 0, stop=a == 1)
                ins.then_inc(c_mm, 1)
            lookup(4, NCH)
            pe.wait_ge(c_ready, 6)
            pe.wait_ge(mlp_in, MLP)
            pe.wait_ge(zeroed, 6)
            pe.wait_ge(lo_done, 1)
            for g in range(QUADS):
                transpose_x(g, "pro", 0)
            transpose_e("pro", 0, 0, 1)
            spread_e("pro", 0)

            def step(i, s, u, phase):
                after = {4: ["a0"], 6: ["a1"], 8: ["a2"], 10: ["a3"], 12: ["C0", "b0"], 13: ["b1"], 15: ["y"],
                         16: ["x0"], 17: ["x1"], 18: ["x2"], 19: ["x3"]}
                for b in range(PB):
                    spread_x(b, s, u, phase)
                    for piece in after.get(b, []):
                        if piece == "C0":
                            contract(0, s)
                        elif piece[0] == "x":
                            if phase != "last":
                                pe.wait_ge(lo_done, s + 2)
                                transpose_x(int(piece[1]), phase, s)
                        elif phase != "first":
                            mlp(piece, phase, s, s - 1)
                if phase != "last":
                    transpose_e(phase, s, 1 - u, i + 1)
                contract(1, s)
                if phase != "last":
                    spread_e(phase, s)

            step(0, 0, 0, "first")
            with pe.Fori(0, LOOPS) as i:
                step(i + 1, 2 * i + 1, 1, "mid")
                step(i + 1, 2 * i + 2, 0, "mid")
            step(0, STEPS - 1, 1, "last")
            for name in ORDER["end"]:
                mlp(name, "end", 0, STEPS - 1)


def shape_constants():
    import numpy as np
    con, conb = np.zeros((P, C_END), np.float32), np.zeros((P, B_END), np.float32)
    con[:, C_ID:C_ID + P] = np.eye(P)
    conb[:, B_ID:B_ID + P] = np.eye(P)
    for f in range(F):
        c = f // 16
        for row0 in ([8 * (f - 16 * c)] if c < 2 else [8 * (f - 32), 64 + 8 * (f - 32)]):
            for i in range(NW):
                row, at = row0 + i, WINDOW[f] + i
                t, d = at // D, at % D
                for part in range(3):
                    conb[part * F + f, B_SX + c * P + row] = 1
                if t in DENSE:
                    n = OH_TERMS.index((c, DENSE.index(t) // 2))
                    for part in range(3):
                        conb[64 * (DENSE.index(t) % 2) + D * part + d, B_SO + n * P + row] = 1
                else:
                    g = GATHERED.index(t) * D + d
                    con[g % P, C_SE + E_TERMS.index((c, g // P)) * P + row] = 1
        m, f8 = f // 8, f % 8
        for i in range(NW):
            for j in range(16):
                for d in range(D):
                    if (256 * f + 16 * j + d) // F == WINDOW[f] + i:
                        conb[16 * f8 + j, B_MD + (m * D + d) * 64 + 8 * f8 + i] = 1
    for p in range(P):
        for a in range(2):
            con[p, C_BD + 16 * a + 8 * a + p // 16] = 1
    for t in DENSE:
        for c in range(CHUNKS[t]):
            con[:VP, C_ROW + CHUNK0[t] + c] = np.arange(VP) * CHUNKS[t] + c
    return con, conb.astype(mybir.dt.np(BF16))


def kernel(**inputs):
    import numpy as _np
    import concourse.bacc as _bacc
    from concourse.bass_utils import run_bass_kernel_spmd as _run

    nc = _bacc.Bacc("TRN2", target_bir_lowering=False, num_devices=1)
    arrays, T = {}, {}
    const, const_b = shape_constants()
    inputs = {**inputs, "const": const, "const_b": const_b, "dense_ctx_t": _np.asarray(inputs["dense_ctx"]).T,
              "ids_t": _np.asarray(inputs["ids"]).T}
    for name in inputs:
        a = _np.ascontiguousarray(inputs[name])
        arrays[f"in_{name}_dram"] = a
        T[name] = nc.dram_tensor(f"in_{name}_dram", a.shape, mybir.dt.from_np(a.dtype), kind="ExternalInput").ap()
    out = nc.dram_tensor("out_0_dram", (B, 1), F32, kind="ExternalOutput").ap()
    interaction_tower(nc, T, out)
    r = _run(nc, [arrays], core_ids=[0])
    return r.results[0]["out_0_dram"]
```

```python
import concourse.bass as bass
from concourse import mybir
from contextlib import ExitStack

F32 = mybir.dt.float32
BF16 = mybir.dt.bfloat16
I32 = mybir.dt.int32
F16 = mybir.dt.float16
ALU = mybir.AluOpType
ACT = mybir.ActivationFunctionType

P = 128
B = 2048
NT, D = 16, 16
NE = NT * D
F, H, K = 39, 16, 16
NW = 8
N1, N2 = 512, 256
SUB = 2
W = SUB * P
STEPS = B // W
LOOPS = (STEPS - 2) // 2
NXR, NSC = 5, 2
NOH = 10
QUADS = H // 4
PB = 5 * QUADS
HALF = PB // 2
X3 = 3 * F

VOCAB = [1000, 1250, 125000, 12500, 1250, 1250, 12500, 125000, 12500, 1000, 125000, 12500, 12500, 125000, 125000, 1000]
DENSE_PAIRS = [(0, 1), (9, 15)]
DENSE = [t for pair in DENSE_PAIRS for t in pair]
NPAIR, NDENSE = len(DENSE_PAIRS), len(DENSE)
GATHERED = [14, 2, 3, 4, 5, 6, 7, 8, 10, 11, 12, 13]
E_WINDOWS = [[14, 2, 3, 4, 5, 6, 13], [6, 7, 8, 10, 11, 12, 13]]
E_WINDOW_OF = [0, 1, 0]
A_COLS = D * 6
B_COL = GATHERED.index(6) * D
NG = len(GATHERED) * D
VP = 125
CHUNKS = {t: VOCAB[t] // VP for t in DENSE}
CHUNK0 = {t: sum(CHUNKS[v] for v in DENSE[:n]) for n, t in enumerate(DENSE)}
NCH = sum(CHUNKS.values())
NA = 5
WINDOW = [min((NE * f) // F, NE - NW) for f in range(F)]


def meets(tables):
    return [c for c in range(3) if any((WINDOW[f] + i) // D in tables for f in range(16 * c, min(16 * c + 16, F)) for i in range(NW))]


assert sorted(GATHERED + DENSE) == list(range(NT))
assert all(t in E_WINDOWS[E_WINDOW_OF[c]] for t in GATHERED for c in meets([t]))
OH_TERMS = [(c, n) for c in range(3) for n in range(NPAIR) if c in meets(DENSE_PAIRS[n])]
NOT = len(OH_TERMS)

DENSE_PARTS = [(0, 0), (0, 1), (0, 2), (1, 0), (2, 0), (2, 1), (1, 1), (1, 2)]
LOW = slice(4 * D, 6 * D)
DW = B + 2 * N1

C_ID, C_SE, C_BD, C_ROW = 0, P, 4 * P, 4 * P + K
C_DN = C_ROW + NCH
C_END = C_DN + 4
B_SX, B_SO, B_ID = 0, 3 * P, (3 + NOT) * P
B_END = B_ID + P
DG, DD = 4, 4
V_W, V_HV, V_B1 = 0, DD * H, DD * H + DD
V_B2, V_W3 = V_B1 + N1 // P, V_B1 + N1 // P + N2 // P
V_END = V_W3 + N2 // P


def interaction_tower(nc, T, out):
    with ExitStack() as ctx:
        def sb(name, shape, dt=F32):
            return ctx.enter_context(nc.sbuf_tensor(name, shape, dt))

        def sem(name):
            return ctx.enter_context(nc.semaphore(name))

        const = sb("const", [P, C_END])
        ident = const[:, C_ID:C_ID + P]
        sel_e = const[:, C_SE:C_SE + 3 * P].rearrange("p (c r) -> p c r", c=3)
        bd_mask = const[:, C_BD:C_BD + K]
        pick = const[:, C_DN:C_DN + 4]
        vocab_row = const[:, C_ROW:C_ROW + NCH]
        const_b = sb("const_b", [P, B_END], BF16)
        sel_x = const_b[:, B_SX:B_SX + 3 * P].rearrange("p (c r) -> p c r", c=3)
        ident_b = const_b[:, B_ID:B_ID + P]
        sel_o = const_b[:, B_SO:B_SO + NOT * P].rearrange("p (t r) -> p t r", t=NOT)
        sel_a = sb("sel_a", [P, NA, DG, DD * 64], BF16)
        small = sb("small", [P, NA + NCH, D])
        small_rest = sb("small_rest", [P, NA + NCH, D])
        small_parts = sb("small_parts", [P, NA + NCH, 4, D], BF16)
        idx_flat = sb("idx_flat", [P, NDENSE * B // P], I32)
        idx_flat16 = sb("idx_flat16", [P, NDENSE * B // P], F16)
        idx = sb("idx", [VP, NDENSE, B], F16)
        oh_t = sb("oh_t", [P, NPAIR, B], BF16)
        oh_now = sb("oh_now", [P, NPAIR, W], BF16)
        al_t = sb("al_t", [P, 3, DD, P])
        vectors = sb("vectors", [P, V_END])
        w_t = vectors[:, V_W:V_W + DD * H].rearrange("p (d h) -> p d h", d=DD)
        hv_t = vectors[:, V_HV:V_HV + DD]
        b1 = vectors[:, V_B1:V_B1 + N1 // P]
        b2 = vectors[:, V_B2:V_B2 + N2 // P]
        w3 = vectors[:, V_W3:V_W3 + N2 // P]
        w_diag = sb("w_diag", [P, DD, H * K])
        c01 = sb("c01", [P, 2, H, 32])
        c2 = sb("c2", [P, H // 2, 32])
        w1 = sb("w1", [P, 2, N1])
        w2 = sb("w2", [P, N1 // P, N2])
        ids = [sb(f"ids{u}", [P, SUB, NT], I32) for u in range(2)]
        x_in = [sb(f"x_in{u}", [P, SUB, F * H]) for u in range(2)]
        e_nat = [sb(f"e_nat{u}", [P, SUB, NG + D]) for u in range(2)]
        x_parts = sb("x_parts", [P, SUB, H, X3], BF16)
        x_part = [x_parts[:, :, :, n * F:(n + 1) * F] for n in range(3)]
        x_rest = sb("x_rest", [P, SUB, H, F])
        x_t = [sb(f"x_t{u}", [X3, H, W], BF16) for u in range(2)]
        e_t = sb("e_t", [P, 2, W])
        dense_w = sb("dense_w", [P, DW])
        dense_parts = sb("dense_parts", [P, DW], BF16)
        dense_t = sb("dense_t", [P, W], BF16)
        e_rep = sb("e_rep", [P, 3, W])
        prod = sb("prod", [P, PB, 2 * W])
        onehot = [prod[0:VP, 2 * n:2 * n + 2, :].rearrange("p a n -> p (a n)").bitcast(BF16) for n in range(NOH)]
        z = sb("z", [P, 2, W])
        h1 = sb("h1", [P, N1 // P, W])
        h2 = sb("h2", [P, N2 // P, W])
        y = sb("y", [P, B // P])
        y_t = sb("y_t", [B // P, P])

        xr = [ctx.enter_context(nc.psum_tensor(f"xr{k}", [P, 512], F32)) for k in range(NXR)]
        sc = [ctx.enter_context(nc.psum_tensor(f"sc{k}", [P, 512], F32)) for k in range(NSC)]
        zp = ctx.enter_context(nc.psum_tensor("zp", [P, 512], F32))

        AL_BANK = (zp, xr[4], sc[0])
        C_BANK = (zp[:, 0:256], zp[:, 256:512], xr[4][:, 0:256])

        const_in, vectors_in, mlp_in = sem("const_in"), sem("vectors_in"), sem("mlp_in")
        ids_in = [sem(f"ids_in{u}") for u in range(2)]
        x_loaded = [sem(f"x_loaded{u}") for u in range(2)]
        gathered = [sem(f"gathered{u}") for u in range(2)]
        e_read = [sem(f"e_read{u}") for u in range(2)]
        y_out = sem("y_out")
        yt_mm, yt_ready = sem("yt_mm"), sem("yt_ready")
        y_turn = sem("y_turn")
        turn = sem("turn")
        idx_in, idx_cast, idx_out = sem("idx_in"), sem("idx_cast"), sem("idx_out")
        idx_all = [sem(f"idx_all{n}") for n in range(NDENSE)]
        small_in, const_b_in, sel_a_in = sem("small_in"), sem("const_b_in"), sem("sel_a_in")
        small_hi, small_left, small_mid, small_lo = (sem(n) for n in ("small_hi", "small_left", "small_mid", "small_lo"))
        oh_ready = [sem(f"oh_ready{n}") for n in range(NOH)]
        oh_read = [sem(f"oh_read{n}") for n in range(NOH)]
        oh_kept = sem("oh_kept")
        oh_now_ready = sem("oh_now_ready")
        dense_ready = sem("dense_ready")
        dense_in, dense_cast = sem("dense_in"), sem("dense_cast")
        dense_left, dense_split = sem("dense_left"), sem("dense_split")
        zeroed = sem("zeroed")
        diag_ready = sem("diag_ready")
        al_mm, al_ready = sem("al_mm"), sem("al_ready")
        c_mm, c_ready = sem("c_mm"), sem("c_ready")
        hi_done, rest_done, mid_done, lo_done = sem("hi_done"), sem("rest_done"), sem("mid_done"), sem("lo_done")
        sc_full = [sem(f"sc_full{k}") for k in range(NSC)]
        sc_free = [sem(f"sc_free{k}") for k in range(NSC)]
        xr_full = [sem(f"xr_full{k}") for k in range(NXR)]
        mult = [sem(f"mult{k}") for k in range(NXR)]
        contracted = [sem(f"contracted{a}") for a in range(2)]
        z_ready = sem("z_ready")

        MLP = 16 * 2

        ONE = 1

        PIECES = [0, 1, "eT", 2, 3, 4, "e", "a0", 5, 6, "a1", 7, 8, "x0", 9, "b0", 10, 11, "x1", 12, 13, 14, "C0",
                  15, 16, 17, 18, 19, "x2", "b1", "x3", "C1", "y"]
        LAST_PIECES = [0, 1, 2, "a0", "eT", 3, 4, "e", "a1", 5, 6, 7, 8, "b0", 9, 10, 11, 12, 13, "C0",
                       14, 15, 16, "b1", 17, 18, 19, "C1", "y"]
        MLP_USES = ["a0", "a1", "b0", "b1", "y"]
        MIXED, LAST = ([use for p in pieces if isinstance(p, str) and p[0] != "C" for use in (["e2", "e01"] if p == "e" else [p])]
                       for pieces in (PIECES, LAST_PIECES))
        START = 3
        assert MIXED[:START] == ["eT", "e2", "e01"] and [p for p in PIECES if isinstance(p, int)] == list(range(PB))
        ORDER = {"pro": ["x0", "x1", "x2", "x3"], "first": MIXED, "mid": MIXED, "last": LAST, "end": MLP_USES}
        PER_STEP = len(MIXED)
        assert PER_STEP % NSC == 0 and PB % NXR == 0
        PER_XR = PB // NXR
        USES0 = len(ORDER["pro"])
        AT = {"pro": 0, "first": USES0, "mid": USES0, "last": USES0 + PER_STEP * (STEPS - 1),
              "end": USES0 + PER_STEP * (STEPS - 1) + len(ORDER["last"])}

        def scratch(name, phase, s):
            n = AT[phase] + ORDER[phase].index(name)
            return n % NSC, n // NSC + (PER_STEP // NSC * s if phase == "mid" else 0)

        OH_ORDER = [(t, c) for pair in DENSE_PAIRS for c in range(max(CHUNKS[t] for t in pair)) for t in pair if c < CHUNKS[t]]

        x_dram = T["r_x0"].rearrange("(s j p) f h -> p s j (f h)", p=P, j=SUB)
        ids_dram = T["ids"].rearrange("(s j p) t -> p s j t", p=P, j=SUB)

        idx_dram = nc.dram_tensor("idx16", [NDENSE, B], F16, kind="Internal").ap()

        block = ctx.enter_context(nc.Block())

        @block.sync
        def _(sp):
            def load_ids(s, u):
                sp.dma_start(ids[u][:], ids_dram[:, bass.ds(s, 1)].rearrange("p o j t -> p (o j) t")).then_inc(ids_in[u], 16)

            def load_x(s, u):
                sp.dma_start(x_in[u][:], x_dram[:, bass.ds(s, 1)].rearrange("p o j c -> p (o j) c")).then_inc(x_loaded[u], 16)

            sp.dma_start(idx_flat[:], T["small_ids"].rearrange("t (a n) -> (t a) n", a=P // NDENSE)).then_inc(idx_in, 16)
            load_ids(0, 0)
            sp.dma_start(small[:], T["alpha_and_tables"]).then_inc(small_in, 16)
            sp.dma_start(const[:], T["const"]).then_inc(const_in, 16)
            sp.wait_ge(idx_cast, 1)
            sp.dma_start(idx_dram.rearrange("t (a n) -> (t a) n", a=P // NDENSE), idx_flat16[:]).then_inc(idx_out, 16)
            load_x(0, 0)
            sp.dma_start(const_b[:], T["const_b"]).then_inc(const_b_in, 16)
            sp.wait_ge(idx_out, 16)

            def load_idx(n):
                sp.dma_start(idx[:, n, :], idx_dram[n:n + 1, :].to_broadcast([VP, B])).then_inc(idx_all[n], 16)

            load_idx(0)
            load_idx(1)
            sp.dma_start(vectors[:], T["vectors"]).then_inc(vectors_in, 16)
            sp.dma_start(sel_a[:].rearrange("p m g r -> p (m g r)"), T["sel_a"]).then_inc(sel_a_in, 16)
            load_idx(2)
            load_idx(3)
            load_ids(1, 1)
            load_x(1, 1)
            sp.dma_start(dense_w[:], T["dense_and_weights"]).then_inc(dense_in, 16)
            sp.dma_start(w1[:], T["W_top1_z"]).then_inc(mlp_in, 16)
            sp.dma_start(w2[:], T["W_top2"].rearrange("(c p) n -> p c n", p=P)).then_inc(mlp_in, 16)

            def ahead(i, u):
                s = 2 * i + u
                sp.wait_ge(gathered[u], 16 * SUB * len(GATHERED) * (i + 1))
                load_ids(s + 2, u)
                sp.wait_ge(rest_done, s + 1)
                load_x(s + 2, u)

            with sp.Fori(0, STEPS // 2 - 1) as i:
                ahead(i, 0)
                ahead(i, 1)

        @block.gpsimd
        def _(pool):
            with pool.Fori(0, STEPS // 2) as i:
                for u in range(2):
                    pool.wait_ge(ids_in[u], 16 * i + 16)
                    pool.wait_ge(e_read[u], i + ONE)
                    pool.sem_inc(turn, 1)
                    for j in range(SUB):
                        for n, t in enumerate(GATHERED):
                            nc.gpsimd.indirect_dma_start(
                                e_nat[u][:, j, n * D:(n + 1) * D], None, T[f"tbl_{t}"],
                                bass.IndirectOffsetOnAxis(ap=ids[u][:, j, t:t + 1], axis=0)).then_inc(gathered[u], 16)

        @block.scalar
        def _(act):
            def hi(i, u):
                act.wait_ge(x_loaded[u], 16 * i + 16)
                nc.scalar.activation(x_part[0], x_in[u][:].rearrange("p j (f h) -> p j h f", h=H),
                                     ACT.Copy).then_inc(hi_done, 1)

            def mid(s):
                act.wait_ge(rest_done, s + 1)
                nc.scalar.activation(x_part[1], x_rest[:], ACT.Copy).then_inc(mid_done, 1)

            act.sem_inc(z_ready, ONE)
            act.wait_ge(small_in, 16)
            act.wait_ge(zeroed, 3)
            nc.scalar.activation(small_parts[:, :, 0, :], small[:], ACT.Copy).then_inc(small_hi, 1)
            act.wait_ge(small_left, 1)
            nc.scalar.activation(small_parts[:, :, 1, :], small_rest[:], ACT.Copy).then_inc(small_mid, 1)
            hi(0, 0)
            mid(0)

            def copy_al():
                for c in range(2):
                    act.wait_ge(al_mm, c + 1)
                    nc.scalar.activation(al_t[:, c], AL_BANK[c][:].rearrange("p (d r) -> p d r", d=DD), ACT.Copy).then_inc(al_ready, 1)
                act.wait_ge(al_mm, 3)
                al2 = AL_BANK[2][:, 0:DD * 64].rearrange("p (d r) -> p d r", d=DD)
                for half in range(2):
                    nc.scalar.activation(al_t[:, 2, :, 64 * half:64 * half + 64], al2, ACT.Copy).then_inc(al_ready, 1)

            def copy_c():
                act.wait_ge(c_mm, 3)
                act.wait_ge(zeroed, 5)
                for c in range(3):
                    c_ps = C_BANK[c].rearrange("p (q a k) -> p q a k", a=2, k=K)
                    for a in range(2):
                        if c < 2:
                            dst = c01[:, c].rearrange("p (q a) k -> p q a k", a=2)[:, :, a, 16 * a:16 * a + 16]
                            src = c_ps[:, :, a, :]
                        else:
                            dst = c2[64 * a:64 * a + 64, :, 16 * a:16 * a + 16]
                            src = c_ps[64 * a:64 * a + 64, :, a, :]
                        nc.scalar.activation(dst, src, ACT.Copy).then_inc(c_ready, 1)

            def keep(n, banks):
                last = max(k for k in range(NCH) if OH_ORDER[k][0] in DENSE_PAIRS[n])
                act.wait_ge(oh_read[last % NOH], last // NOH + 1)
                for g in banks:
                    nc.scalar.activation(oh_t[:, n, g * 512:(g + 1) * 512], xr[g][:], ACT.Copy).then_inc(oh_kept, 1)

            def dense_slice(s):
                nc.scalar.activation(dense_t[:], dense_parts[:, bass.ts(s, W)], ACT.Copy).then_inc(dense_ready, 1)

            def oh_slice(s):
                nc.scalar.activation(oh_now[:], oh_t[:, :, bass.ts(s, W)], ACT.Copy).then_inc(oh_now_ready, 1)

            def empty(name, phase, s, u):
                k, before = scratch(name, phase, s)
                bank, free, m = sc[k], sc_free[k], int(name[1]) if name[0] in "abx" else 0
                act.wait_ge(sc_full[k], before + 1)
                if name == "eT":
                    act.sem_inc(e_read[u], 1)
                    nc.scalar.activation(e_t[:], bank[:].rearrange("p (a n) -> p a n", a=2), ACT.Copy).then_inc(free, 1)
                elif name == "e01":
                    nc.scalar.activation(e_rep[:, 0:2, :], bank[:].rearrange("p (a n) -> p a n", a=2), ACT.Copy).then_inc(free, 1)
                elif name == "e2":
                    nc.scalar.activation(e_rep[:, 2, :], bank[:, 0:W], ACT.Copy).then_inc(free, 1)
                elif name[0] == "x":
                    dst = x_t[u if phase == "pro" else 1 - u][:, 4 * m:4 * m + 4, :]
                    src = bank[0:X3, :].bitcast(BF16).rearrange("p (h n) -> p h n", h=4)
                    nc.scalar.activation(dst, src, ACT.Copy).then_inc(free, 1)
                elif name[0] == "a":
                    nc.scalar.activation(h1[:, 2 * m, :], bank[:, 0:W], ACT.Relu, bias=b1[:, 2 * m:2 * m + 1])
                    nc.scalar.activation(h1[:, 2 * m + 1, :], bank[:, W:2 * W], ACT.Relu, bias=b1[:, 2 * m + 1:2 * m + 2]).then_inc(free, 1)
                elif name[0] == "b":
                    nc.scalar.activation(h2[:, m, :], bank[:, 0:W], ACT.Relu, bias=b2[:, m:m + 1]).then_inc(free, 1)
                else:
                    act.sem_inc(y_turn, 1)
                    done = {"mid": s - 1, "last": STEPS - 2, "end": STEPS - 1}[phase]
                    nc.scalar.activation(y[:, bass.ts(done, SUB)], bank[:, 0:SUB], ACT.Copy).then_inc(free, 1)

            def copy_z(s):
                act.wait_ge(contracted[1], s + 1 + ONE)
                nc.scalar.activation(z[:], zp[:].rearrange("p (a n) -> p a n", a=2), ACT.Copy).then_inc(z_ready, 1)

            def pass_over(name, s):
                k, before = scratch(name, "first", s)
                act.wait_ge(sc_full[k], before + 1)
                act.sem_inc(sc_free[k], 1)

            def step(i, s, u, phase):
                for name in ORDER[phase][START if phase == "first" else 0:]:
                    if name == "a0" and phase == "mid":
                        mid(s + 1)
                    if name == "y":
                        copy_z(s)
                    if phase == "first" and name in MLP_USES:
                        pass_over(name, s)
                    else:
                        empty(name, phase, s, u)
                    if name == "eT" and phase == "mid":
                        hi(i, 1 - u)
                    if name == ("b0" if phase == "last" else "x0"):
                        if phase != "first":
                            dense_slice(s)
                        if phase != "last":
                            oh_slice(s + 1)
                    if phase == "first" and name == "x3":
                        act.wait_ge(dense_left, 3)
                        nc.scalar.activation(dense_parts[:], dense_w[:], ACT.Copy).then_inc(dense_cast, 1)

            for name in ORDER["pro"]:
                empty(name, "pro", 0, 0)
            copy_al()
            hi(0, 1)
            keep(0, range(4))
            copy_c()
            mid(1)
            act.wait_ge(dense_in, 16)
            nc.scalar.activation(dense_parts[:], dense_w[:], ACT.Copy).then_inc(dense_cast, 1)
            act.wait_ge(oh_kept, 4)
            nc.scalar.activation(oh_now[:, 0, :], oh_t[:, 0, 0:W], ACT.Copy)
            empty("eT", "first", 0, 0)
            act.wait_ge(oh_read[(NCH - 1) % NOH], (NCH - 1) // NOH + 1)
            nc.scalar.activation(oh_now[:, 1, :], xr[0][:, 0:W], ACT.Copy).then_inc(oh_now_ready, 1)
            keep(1, range(1))
            empty("e2", "first", 0, 0)
            empty("e01", "first", 0, 0)
            act.wait_ge(mlp_in, MLP)
            step(0, 0, 0, "first")
            with act.Fori(0, LOOPS) as i:
                step(i + 1, 2 * i + 1, 1, "mid")
                step(i + 1, 2 * i + 2, 0, "mid")
            step(0, STEPS - 1, 1, "last")
            for name in ORDER["end"]:
                empty(name, "end", 0, 0)
            act.wait_ge(yt_mm, 1)
            nc.scalar.activation(y_t[:], zp[0:B // P, 0:P], ACT.Copy).then_inc(yt_ready, 1)
            act.wait_ge(yt_ready, 1)
            act.dma_start(out.rearrange("(c p) o -> c (p o)", p=P), y_t[:]).then_inc(y_out, 16)
            act.wait_ge(y_out, 16)

        @block.vector
        def _(dve):
            def rest(i, u, s):
                dve.wait_ge(hi_done, s + 1)
                dve.wait_ge(x_loaded[u], 16 * i + 16)
                nc.vector.tensor_tensor(x_rest[:], x_in[u][:].rearrange("p j (f h) -> p j h f", h=H),
                                        x_part[0], ALU.subtract).then_inc(rest_done, 1)

            def low(u, s):
                dve.wait_ge(mid_done, s + 1)
                nc.vector.tensor_tensor(x_part[2], x_rest[:], x_part[1],
                                        ALU.subtract).then_inc(lo_done, 1)

            def diagonal():
                dve.wait_ge(vectors_in, 16)
                for dd in range(DD):
                    nc.vector.scalar_tensor_tensor(
                        out=w_diag[:, dd].rearrange("p (h k) -> p h k", k=K),
                        in0=w_t[:, dd].rearrange("p (h o) -> p h o", o=1).to_broadcast([P, H, K]), scalar=hv_t[:, dd:dd + 1],
                        in1=bd_mask.rearrange("p (o k) -> p o k", o=1).to_broadcast([P, H, K]), op0=ALU.mult, op1=ALU.mult).then_inc(diag_ready, 1)

            def dense_less(n, out, done):
                dve.wait_ge(dense_cast, n + 1)
                for cols, factor in ((slice(0, B), pick[:, n:n + 1]), (slice(B, B + N1), pick[:, 2 + n:3 + n]), (slice(B + N1, DW), -1.0)):
                    nc.vector.scalar_tensor_tensor(out=out[:, cols], in0=dense_parts[:, cols], scalar=factor, in1=dense_w[:, cols],
                                                   op0=ALU.mult, op1=ALU.add).then_inc(done, 1)

            for k in range(NXR):
                dve.sem_inc(mult[k], ONE)
            nc.vector.memset(small_parts[:, :, 3, :], 0.0).then_inc(zeroed, 1)
            for u in range(2):
                nc.vector.memset(e_nat[u][:, :, NG:], 0.0).then_inc(zeroed, 1)
            dve.wait_ge(idx_in, 16)
            nc.vector.tensor_copy(idx_flat16[:], idx_flat[:]).then_inc(idx_cast, 1)
            nc.vector.memset(c01[:], 0.0).then_inc(zeroed, 1)
            nc.vector.memset(c2[:], 0.0).then_inc(zeroed, 1)
            dve.wait_ge(small_hi, 1)
            nc.vector.tensor_tensor(small_rest[:], small[:], small_parts[:, :, 0, :], ALU.subtract).then_inc(small_left, 1)
            dve.wait_ge(small_mid, 1)
            nc.vector.tensor_tensor(small_parts[:, :, 2, :], small_rest[:], small_parts[:, :, 1, :], ALU.subtract).then_inc(small_lo, 1)
            rest(0, 0, 0)
            dve.wait_ge(const_in, 16)
            for n, (t, c) in enumerate(OH_ORDER):
                if c == 0:
                    dve.wait_ge(idx_all[DENSE.index(t)], 16)
                if n >= NOH:
                    dve.wait_ge(oh_read[n % NOH], n // NOH)
                row = CHUNK0[t] + c
                nc.vector.tensor_scalar(onehot[n % NOH], idx[:, DENSE.index(t), :], vocab_row[0:VP, row:row + 1], None,
                                        ALU.is_equal).then_inc(oh_ready[n % NOH], 1)
                if n == 1:
                    low(0, 0)
                if n == 9:
                    diagonal()
                if n == 27:
                    rest(0, 1, 1)
                if n == 29:
                    low(1, 1)
            dve.wait_ge(oh_read[(NCH - 1) % NOH], (NCH - 1) // NOH + 1)
            for g in range(1, 4):
                nc.vector.tensor_copy(oh_t[:, NPAIR - 1, g * 512:(g + 1) * 512], xr[g][:]).then_inc(oh_kept, 1)

            def step(i, s, u, phase):
                if phase == "mid":
                    rest(i, 1 - u, s + 1)
                for name in ("e01", "e2"):
                    k, before = scratch(name, phase, s)
                    dve.wait_ge(sc_free[k], before + 1)
                for b in range(PB):
                    k, q = b % NXR, b // NXR
                    c = (b % 5) // 2
                    dve.wait_ge(xr_full[k], PER_XR * s + q + 1)
                    if b % HALF == 0:
                        dve.wait_ge(contracted[b // HALF], s + ONE)
                    nc.vector.tensor_tensor(prod[:, b, :].rearrange("p (a n) -> p a n", a=2),
                                            xr[k][:].rearrange("p (a n) -> p a n", a=2),
                                            e_rep[:, c:c + 1, :].to_broadcast([P, 2, W]), ALU.mult).then_inc(mult[k], 1)
                    if phase == "mid" and b == 2:
                        low(1 - u, s + 1)
                    if phase == "first" and b == 9:
                        dense_less(0, dense_w, dense_left)
                if phase == "first":
                    dense_less(1, dense_parts, dense_split)
                    dve.wait_ge(dense_split, 3)
                    nc.vector.tensor_copy(dense_t[:], dense_parts[:, 0:W]).then_inc(dense_ready, 1)

            step(0, 0, 0, "first")
            with dve.Fori(0, LOOPS) as i:
                step(i + 1, 2 * i + 1, 1, "mid")
                step(i + 1, 2 * i + 2, 0, "mid")
            step(0, STEPS - 1, 1, "last")

        @block.tensor
        def _(pe):
            def fill(name, phase, s):
                k, before = scratch(name, phase, s)
                if not (phase == "pro" and before == 0):
                    pe.wait_ge(sc_free[k], before)
                return sc[k], sc_full[k]

            def emptied(name, phase, s):
                k, before = scratch(name, phase, s)
                pe.wait_ge(sc_free[k], before + 1)

            def transpose_x(g, phase, s):
                bank, full = fill(f"x{g}", phase, s)
                for h in range(4):
                    for j in range(SUB):
                        ins = nc.tensor.transpose(bank[0:X3, :].bitcast(BF16)[:, (h * SUB + j) * P:(h * SUB + j + 1) * P],
                                                  x_parts[:, j, 4 * g + h], ident_b)
                ins.then_inc(full, 1)

            def transpose_e(phase, s, u, count):
                pe.wait_ge(gathered[u], 16 * SUB * len(GATHERED) * count)
                bank, full = fill("eT", phase, s)
                for j in range(SUB):
                    first, second = bank[:, j * P:(j + 1) * P], bank[:, (SUB + j) * P:(SUB + j + 1) * P]
                    nc.tensor.transpose(first[0:A_COLS], e_nat[u][:, j, 0:A_COLS], ident)
                    nc.tensor.matmul(first[A_COLS:P], e_nat[u][:, j, NG - D:NG + D], ident, start=True, stop=True)
                    ins = nc.tensor.transpose(second, e_nat[u][:, j, B_COL:B_COL + P], ident)
                ins.then_inc(full, 1)

            def spread_e(phase, s):
                emptied("eT", phase, s)
                for name, chunks in (("e2", (2,)), ("e01", (0, 1))):
                    bank, full = fill(name, phase, s)
                    for c in chunks:
                        terms = [(sel_e[:, c, :], e_t[:, E_WINDOW_OF[c], :])]
                        terms += [(sel_o[:, n, :], oh_now[:, a, :]) for n, (cc, a) in enumerate(OH_TERMS) if cc == c]
                        for n, (sel, e) in enumerate(terms):
                            if c == 2 and n == 1:
                                pe.wait_ge(oh_now_ready, s + 1)
                            ins = nc.tensor.matmul(bank[:, (c % 2) * W:(c % 2 + 1) * W], sel, e, start=n == 0, stop=n == len(terms) - 1)
                    ins.then_inc(full, 1)

            def spread_x(b, s, u, phase):
                k, q = b % NXR, b // NXR
                if b % 5 == 0:
                    emptied(f"x{b // 5}", *(("pro", 0) if phase == "first" else ("mid", s - 1)))
                pe.wait_ge(mult[k], PER_XR * s + q + ONE)
                h0, r = 4 * (b // 5), b % 5
                if r < 4:
                    h = h0 + 2 * (r % 2)
                    ins = nc.tensor.matmul(xr[k][:], sel_x[0:X3, r // 2, :], x_t[u][0:X3, h:h + 2, :], start=True, stop=True)
                else:
                    for hh in range(2):
                        ins = nc.tensor.matmul(xr[k][64 * hh:64 * hh + 64, :], sel_x[0:X3, 2, 0:64],
                                               x_t[u][0:X3, h0 + hh:h0 + 4:2, :], start=True, stop=True)
                ins.then_inc(xr_full[k], 1)

            def contract(half, s):
                if half == 0:
                    pe.wait_ge(z_ready, s + ONE)
                for m in range(5):
                    if m % 2 == 0:
                        for b in range(HALF * half + 5 + m, HALF * half + min(7 + m, 10)):
                            pe.wait_ge(mult[b % NXR], PER_XR * s + b // NXR + 1 + ONE)
                    for q in range(4):
                        base, pp = 5 * (2 * half + q // 2), q % 2
                        pair = 4 * half + q
                        if m < 4:
                            c, a = m // 2, m % 2
                            lhs = c01[:, c, 2 * pair + a, :]
                            rhs = prod[:, base + 2 * c + pp, a * W:(a + 1) * W]
                        else:
                            lhs, rhs = c2[:, pair, :], prod[:, base + 4, pp * W:(pp + 1) * W]
                        ins = nc.tensor.matmul(zp[32 * q:32 * q + 32, half * W:(half + 1) * W], lhs, rhs,
                                               start=m == 0, stop=m == 4)
                ins.then_inc(contracted[half], 1)

            def first_layer(g, phase, s, done):
                bank, full = fill(f"a{g}", phase, s)
                pe.wait_ge(dense_ready, done + 1)
                for mm in range(2):
                    part, cols = slice(mm * W, (mm + 1) * W), slice((2 * g + mm) * P, (2 * g + mm + 1) * P)
                    w_at = B + (2 * g + mm) * P
                    nc.tensor.matmul(bank[:, part], dense_parts[:, w_at:w_at + P], dense_t[:], start=True, stop=False)
                    nc.tensor.matmul(bank[:, part], dense_parts[LOW, N1 + w_at:N1 + w_at + P], dense_t[LOW, :], start=False, stop=False)
                    if mm == 0:
                        pe.wait_ge(z_ready, done + 1 + ONE)
                    for a in range(2):
                        ins = nc.tensor.matmul(bank[:, part], w1[:, a, cols], z[:, a, :], start=False, stop=a == 1)
                ins.then_inc(full, 1)

            def second_layer(m, phase, s):
                bank, full = fill(f"b{m}", phase, s)
                for c in range(N1 // P):
                    if c % 2 == 0:
                        emptied(f"a{c // 2}", phase, s)
                    ins = nc.tensor.matmul(bank[:, 0:W], w2[:, c, m * P:(m + 1) * P], h1[:, c, :], start=c == 0, stop=c == N1 // P - 1)
                ins.then_inc(full, 1)

            def third_layer(phase, s):
                bank, full = fill("y", phase, s)
                emptied("b1", phase, s)
                for j in range(SUB):
                    for c in range(N2 // P):
                        ins = nc.tensor.matmul(bank[:, j:j + 1], h2[:, c, j * P:(j + 1) * P], w3[:, c:c + 1], start=c == 0, stop=c == N2 // P - 1)
                ins.then_inc(full, 1)

            for a in range(2):
                pe.sem_inc(e_read[a], ONE)
                pe.sem_inc(contracted[a], ONE)

            def sum_alpha(m):
                c, half = m // 2, m % 2
                rows = min(P, F * 16 - m * P)
                for g in range(DG):
                    dst = AL_BANK[c][32 * g:32 * g + 32, 0:DD * (P if c < 2 else 64)].rearrange("p (d r) -> p d r", d=DD)
                    for part in range(3):
                        ins = nc.tensor.matmul(dst[:, :, 64 * half:64 * half + 64],
                                               small_parts[0:rows, m, part:part + 2, :].rearrange("p a k -> p (a k)"),
                                               sel_a[0:rows, m, g].rearrange("p (d r) -> p d r", d=DD), start=part == 0, stop=part == 2)
                if half == 1 or m == NA - 1:
                    ins.then_inc(al_mm, 1)

            def sum_c(c):
                for dd in range(DD):
                    ins = nc.tensor.matmul(C_BANK[c], al_t[:, c, dd, :], w_diag[:, dd, :], start=dd == 0, stop=dd == DD - 1)
                ins.then_inc(c_mm, 1)

            def pass_over(name, s):
                _, full = fill(name, "first", s)
                pe.sem_inc(full, 1)

            def lookup(n0, n1):
                for n in range(n0, n1):
                    t, c = OH_ORDER[n]
                    pair = DENSE.index(t) // 2
                    side = DENSE.index(t) % 2
                    pe.wait_ge(oh_ready[n % NOH], n // NOH + 1)
                    if pair > 0 and c == 0:
                        pe.wait_ge(oh_kept, 4 * pair)
                    for g in range(4):
                        parts = small_parts[0:VP, NA + CHUNK0[t] + c].rearrange("p a d -> p (a d)")
                        ins = nc.tensor.matmul(xr[g][64 * side:64 * side + 64, :], parts,
                                               onehot[n % NOH][:, g * 512:(g + 1) * 512], start=c == 0, stop=c == CHUNKS[t] - 1)
                    ins.then_inc(oh_read[n % NOH], 1)

            pe.wait_ge(zeroed, 5)
            pe.wait_ge(small_lo, 1)
            at_x, at_al, at_c, at_e = {2: 0, 3: 1, 4: 2, 5: 3}, {6: 0, 7: 1, 8: 2, 9: 3, 10: 4}, {13: 0, 15: 1, 17: 2}, 26
            for n in range(NCH):
                lookup(n, n + 1)
                if n in at_x:
                    if at_x[n] == 0:
                        pe.wait_ge(const_b_in, 16)
                        pe.wait_ge(lo_done, 1)
                    transpose_x(at_x[n], "pro", 0)
                if n in at_al:
                    if at_al[n] == 0:
                        pe.wait_ge(sel_a_in, 16)
                    if at_al[n] == NA - 1:
                        emptied("x2", "pro", 0)
                    sum_alpha(at_al[n])
                if n in at_c:
                    if at_c[n] == 0:
                        pe.wait_ge(al_ready, 4)
                        pe.wait_ge(diag_ready, DD)
                    sum_c(at_c[n])
                if n == at_e:
                    pe.wait_ge(const_in, 16)
                    transpose_e("first", 0, 0, 1)
            spread_e("first", 0)
            pe.wait_ge(oh_kept, 4 * NPAIR)
            pe.wait_ge(c_ready, 6)
            pe.wait_ge(mlp_in, MLP)

            def step(n, s, u, phase):
                for piece in LAST_PIECES if phase == "last" else PIECES:
                    if isinstance(piece, int):
                        spread_x(piece, s, u, phase)
                    elif phase == "first" and piece in ("eT", "e"):
                        continue
                    elif piece[0] == "C":
                        contract(int(piece[1]), s)
                    elif phase == "first" and piece in MLP_USES:
                        pass_over(piece, s)
                    elif piece[0] == "a":
                        first_layer(int(piece[1]), phase, s, s - 1)
                    elif piece[0] == "b":
                        second_layer(int(piece[1]), phase, s)
                    elif piece == "y":
                        third_layer(phase, s)
                    elif piece == "eT":
                        transpose_e(phase, s, u, n)
                    elif piece == "e":
                        spread_e(phase, s)
                    else:
                        pe.wait_ge(lo_done, s + 2)
                        transpose_x(int(piece[1]), phase, s)

            step(1, 0, 0, "first")
            with pe.Fori(0, LOOPS) as i:
                step(i + 1, 2 * i + 1, 1, "mid")
                step(i + 2, 2 * i + 2, 0, "mid")
            step(STEPS // 2, STEPS - 1, 1, "last")
            for m in range(2):
                first_layer(m, "end", 0, STEPS - 1)
            for m in range(2):
                second_layer(m, "end", 0)
            third_layer("end", 0)
            emptied("y", "end", 0)
            nc.tensor.transpose(zp[0:B // P, 0:P], y[:], ident).then_inc(yt_mm, 1)


def shape_constants():
    import numpy as np
    con, conb = np.zeros((P, C_END), np.float32), np.zeros((P, B_END), np.float32)
    sel = np.zeros((P, NA, DG, DD, 64), np.float32)
    con[:, C_ID:C_ID + P] = np.eye(P)
    conb[:, B_ID:B_ID + P] = np.eye(P)
    for f in range(F):
        c = f // 16
        for row0 in ([8 * (f - 16 * c)] if c < 2 else [8 * (f - 32), 64 + 8 * (f - 32)]):
            for i in range(NW):
                row, at = row0 + i, WINDOW[f] + i
                t, d = at // D, at % D
                for part in range(3):
                    conb[part * F + f, B_SX + c * P + row] = 1
                if t in DENSE:
                    n = OH_TERMS.index((c, DENSE.index(t) // 2))
                    for part in range(3):
                        conb[64 * (DENSE.index(t) % 2) + D * part + d, B_SO + n * P + row] = 1
                else:
                    rows = E_WINDOWS[E_WINDOW_OF[c]]
                    con[rows.index(t) * D + d, C_SE + c * P + row] = 1
        m, f8 = f // 8, f % 8
        for i in range(NW):
            for j in range(16):
                for d in range(D):
                    if (256 * f + 16 * j + d) // F == WINDOW[f] + i:
                        sel[16 * f8 + j, m, d // DD, d % DD, 8 * f8 + i] = 1
    for g in range(DG):
        for k in range(K):
            con[32 * g + k, C_BD + k] = 1
    for t in DENSE:
        for c in range(CHUNKS[t]):
            con[:VP, C_ROW + CHUNK0[t] + c] = np.arange(VP) * CHUNKS[t] + c
    for n, parts in enumerate(DENSE_PARTS):
        for side, part in enumerate(parts):
            for less in range(part):
                con[D * n:D * n + D, C_DN + 2 * side + less] = -1
    return con, conb.astype(mybir.dt.np(BF16)), sel.reshape(P, -1).astype(mybir.dt.np(BF16))


def laid_out(inputs):
    import numpy as np
    a = {name: np.asarray(v) for name, v in inputs.items()}
    small = np.zeros((P, NA + NCH, D), np.float32)
    alpha = a["L0_rec_alpha"]
    for m in range(NA):
        rows = alpha[m * P:(m + 1) * P]
        small[:len(rows), m] = rows
    for t in DENSE:
        small[:VP, NA + CHUNK0[t]:NA + CHUNK0[t] + CHUNKS[t]] = a[f"tbl_{t}"].reshape(VP, CHUNKS[t], D)
    vectors = np.zeros((P, V_END), np.float32)
    for g in range(DG):
        cols = slice(DD * g, DD * g + DD)
        vectors[32 * g:32 * g + K, V_W:V_W + DD * H] = a["L0_rec_w"][:, :, cols].transpose(0, 2, 1).reshape(K, DD * H)
        vectors[32 * g:32 * g + K, V_HV:V_HV + DD] = a["L0_rec_hv"][:, cols, 0]
    for at, name in ((V_B1, "b_top1"), (V_B2, "b_top2"), (V_W3, "W_top3")):
        cols = a[name].reshape(-1, P).T
        vectors[:, at:at + cols.shape[1]] = cols
    w1 = a["W_top1"][0:NE].reshape(K, 2, H // 2, N1).transpose(2, 0, 1, 3).reshape(P, 2, N1)
    dense_w = np.zeros((P, DW), np.float32)
    for n in range(len(DENSE_PARTS)):
        dense_w[D * n:D * n + D, :B] = a["dense_ctx"].T
        dense_w[D * n:D * n + D, B:B + N1] = a["W_top1"][NE:]
    dense_w[LOW.start:LOW.start + D, B + N1:] = a["W_top1"][NE:]
    return {"alpha_and_tables": small, "vectors": vectors, "W_top1_z": w1, "dense_and_weights": dense_w,
            "small_ids": a["ids"][:, DENSE].T}


def kernel(**inputs):
    import numpy as _np
    import concourse.bacc as _bacc
    from concourse.bass_utils import run_bass_kernel_spmd as _run

    nc = _bacc.Bacc("TRN2", target_bir_lowering=False, num_devices=1)
    arrays, T = {}, {}
    const, const_b, sel_a = shape_constants()
    inputs = {**inputs, **laid_out(inputs), "const": const, "const_b": const_b, "sel_a": sel_a}
    for name in inputs:
        a = _np.ascontiguousarray(inputs[name])
        arrays[f"in_{name}_dram"] = a
        T[name] = nc.dram_tensor(f"in_{name}_dram", a.shape, mybir.dt.from_np(a.dtype), kind="ExternalInput").ap()
    out = nc.dram_tensor("out_0_dram", (B, 1), F32, kind="ExternalOutput").ap()
    interaction_tower(nc, T, out)
    r = _run(nc, [arrays], core_ids=[0])
    return r.results[0]["out_0_dram"]
```
